# Optimizing a Trainium2 kernel written in Bass

```python
import numpy as np
import jax
import jax.numpy as jnp

def _softmax(x, axis=-1):
    return jax.nn.softmax(x, axis=axis)

def _gelu(x):
    return jax.nn.gelu(x, approximate=True)

def _silu(x):
    return jax.nn.silu(x)

def _sigmoid(x):
    return jax.nn.sigmoid(x)

def _layernorm(x, axis=-1, eps=1e-05):
    m = jnp.mean(x, axis=axis, keepdims=True)
    v = jnp.var(x, axis=axis, keepdims=True)
    return (x - m) / jnp.sqrt(v + eps)

def _scatter_add(tgt, idx, src, axis=0):
    return tgt.at[idx].add(src)

def _segment_sum(src, seg, n):
    return jax.ops.segment_sum(src, seg, n)
kernel_name = 'mk_sandwich_d1_jaxref_r8_c9634f'

def setup_inputs(seed: int=0):
    np.random.seed(seed)
    _w = jnp.asarray

    def _L0_attn_setup():
        import jax, jax.numpy as jnp
        import numpy as np
        import math
        DK = 128
        key = jax.random.key(seed)
        k1, k2 = jax.random.split(key)
        x = jax.random.normal(k1, (4, 256, 128), dtype=jnp.float32)
        W = jax.random.normal(k2, (128, 3 * DK), dtype=jnp.float32) * (1.0 / math.sqrt(128))
        b = jnp.zeros((3 * DK,), dtype=jnp.float32)
        return {'x': x, 'W': W, 'b': b}
    _L0_attn_in = _L0_attn_setup()

    def _L0_ffn_setup():
        import jax, jax.numpy as jnp
        import numpy as np
        DIM = 128
        DEPTH = 2
        HEADS = 8
        DIM_HEAD = 64
        WINDOW = 64
        INNER = HEADS * DIM_HEAD
        HID = int(DIM * 4 * 2 / 3)
        B, N = (2, 1024)
        QK_SCALE = 8.0

        def shift_token(t):
            t1, t2 = jnp.split(t, 2, axis=-1)
            t2 = jnp.pad(t2, ((0, 0), (1, 0), (0, 0)))[:, :-1]
            return jnp.concatenate([t1, t2], axis=-1)

        def l2norm(t):
            return t / jnp.clip(jnp.linalg.norm(t, axis=-1, keepdims=True), 1e-12)

        def rotate_half(x):
            x1, x2 = jnp.split(x, 2, axis=-1)
            return jnp.concatenate([-x2, x1], axis=-1)

        def rotary_xpos(q, k):
            n = q.shape[-2]
            half_idx = jnp.arange(0, DIM_HEAD, 2, dtype=jnp.float32)
            inv_freq = 1.0 / 10000.0 ** (half_idx / DIM_HEAD)
            t = jnp.arange(n, dtype=jnp.float32)
            freqs = t[:, None] * inv_freq[None, :]
            freqs = jnp.concatenate([freqs, freqs], axis=-1)
            base = (half_idx + 0.4 * DIM_HEAD) / (1.4 * DIM_HEAD)
            power = (t - n // 2) / float(WINDOW // 2)
            scale = base[None, :] ** power[:, None]
            scale = jnp.concatenate([scale, scale], axis=-1)
            cos, sin = (jnp.cos(freqs), jnp.sin(freqs))
            q = q * cos * scale + rotate_half(q) * sin * scale
            k = k * cos / scale + rotate_half(k) * sin / scale
            return (q, k)

        def local_attention(q, k, v):
            b, h, n, d = q.shape
            w = n // WINDOW
            bq = q.reshape(b, h, w, WINDOW, d) * QK_SCALE
            bk = k.reshape(b, h, w, WINDOW, d)
            bv = v.reshape(b, h, w, WINDOW, d)

            def look_around(t):
                p = jnp.pad(t, ((0, 0), (0, 0), (1, 0), (0, 0), (0, 0)))
                return jnp.concatenate([p[:, :, :w], p[:, :, 1:]], axis=3)
            bk, bv = (look_around(bk), look_around(bv))
            bt = jnp.arange(n).reshape(w, WINDOW)
            btp = jnp.pad(bt, ((1, 0), (0, 0)), constant_values=-1)
            btk = jnp.concatenate([btp[:w], btp[1:]], axis=1)
            sim = jnp.einsum('bhwid,bhwjd->bhwij', bq, bk)
            i = bt[:, :, None]
            j = btk[:, None, :]
            mask = (i < j) | (i > j + WINDOW) | (j == -1)
            sim = jnp.where(mask, -jnp.finfo(sim.dtype).max, sim)
            attn = jax.nn.softmax(sim, axis=-1)
            out = jnp.einsum('bhwij,bhwjd->bhwid', attn, bv)
            return out.reshape(b, h, n, d)

        def _layer(x, wqkv, qs, ksc, wo, lg, lb, w1, b1, w2, b2):
            b, n, _ = x.shape
            h = shift_token(x)
            qkv = h @ wqkv
            q, k, v = jnp.split(qkv, 3, axis=-1)
            to_heads = lambda t: t.reshape(b, n, HEADS, DIM_HEAD).transpose(0, 2, 1, 3)
            q, k, v = (to_heads(q), to_heads(k), to_heads(v))
            q = l2norm(q) * qs
            k = l2norm(k) * ksc
            q, k = rotary_xpos(q, k)
            o = local_attention(q, k, v)
            o = o.transpose(0, 2, 1, 3).reshape(b, n, INNER)
            x = x + o @ wo
            h = shift_token(x)
            mu = h.mean(-1, keepdims=True)
            var = h.var(-1, keepdims=True)
            h = (h - mu) / jnp.sqrt(var + 1e-05) * lg + lb
            h = h @ w1 + b1
            a, g = jnp.split(h, 2, axis=-1)
            h = a * jax.nn.gelu(g, approximate=False)
            x = x + h @ w2 + b2
            return x
        key = jax.random.key(seed)
        ks = jax.random.split(key, 6)
        return {'x': jax.random.normal(ks[0], (B, N, DIM), jnp.float32), 'wqkv': jax.random.normal(ks[1], (DEPTH, DIM, 3 * INNER), jnp.float32) * 0.02, 'q_scale': jnp.ones((DEPTH, DIM_HEAD), jnp.float32), 'k_scale': jnp.ones((DEPTH, DIM_HEAD), jnp.float32), 'wo': jax.random.normal(ks[2], (DEPTH, INNER, DIM), jnp.float32) * 0.02, 'ln_g': jnp.ones((DEPTH, DIM), jnp.float32), 'ln_b': jnp.zeros((DEPTH, DIM), jnp.float32), 'w1': jax.random.normal(ks[3], (DEPTH, DIM, 2 * HID), jnp.float32) * 0.02, 'b1': jnp.zeros((DEPTH, 2 * HID), jnp.float32), 'w2': jax.random.normal(ks[4], (DEPTH, HID, DIM), jnp.float32) * 0.02, 'b2': jnp.zeros((DEPTH, DIM), jnp.float32)}
    _L0_ffn_in = _L0_ffn_setup()
    _d = {'L0_attn_x': _L0_attn_in['x'], 'L0_attn_W': _L0_attn_in['W'], 'L0_attn_b': _L0_attn_in['b'], 'L0_ffn_wqkv': _L0_ffn_in['wqkv'], 'L0_ffn_q_scale': _L0_ffn_in['q_scale'], 'L0_ffn_k_scale': _L0_ffn_in['k_scale'], 'L0_ffn_wo': _L0_ffn_in['wo'], 'L0_ffn_ln_g': _L0_ffn_in['ln_g'], 'L0_ffn_ln_b': _L0_ffn_in['ln_b'], 'L0_ffn_w1': _L0_ffn_in['w1'], 'L0_ffn_b1': _L0_ffn_in['b1'], 'L0_ffn_w2': _L0_ffn_in['w2'], 'L0_ffn_b2': _L0_ffn_in['b2']}
    _x0 = _d['L0_attn_x']
    _d['L0_attn_x'] = jax.random.normal(jax.random.fold_in(jax.random.key(seed), 1), (8, 1024, 128), dtype=_x0.dtype)
    del _x0
    return _d

def reference(L0_attn_x, L0_attn_W, L0_attn_b, L0_ffn_wqkv, L0_ffn_q_scale, L0_ffn_k_scale, L0_ffn_wo, L0_ffn_ln_g, L0_ffn_ln_b, L0_ffn_w1, L0_ffn_b1, L0_ffn_w2, L0_ffn_b2):

    def _L0_attn_ref(x, W, b):
        import jax, jax.numpy as jnp
        import numpy as np
        import math
        DK = 128
        qkv = jnp.einsum('btc,cd->btd', x, W) + b
        q, k, v = jnp.split(qkv, 3, axis=-1)
        scale = 1.0 / math.sqrt(DK)
        weights = jnp.einsum('btc,bTc->btT', q, k) * scale
        T = weights.shape[-1]
        mask = jnp.tril(jnp.ones((T, T), dtype=jnp.float32))
        logits = jnp.where(mask == 0, jnp.float32(-9000000000000000.0), weights)
        attention = jax.nn.softmax(logits, axis=-1)
        values = jnp.einsum('btT,bTc->btc', attention, v)
        return values

    def _L0_ffn_ref(x, wqkv, q_scale, k_scale, wo, ln_g, ln_b, w1, b1, w2, b2):
        import jax, jax.numpy as jnp
        import numpy as np
        DIM = 128
        DEPTH = 2
        HEADS = 8
        DIM_HEAD = 64
        WINDOW = 64
        INNER = HEADS * DIM_HEAD
        HID = int(DIM * 4 * 2 / 3)
        B, N = (2, 1024)
        QK_SCALE = 8.0

        def shift_token(t):
            t1, t2 = jnp.split(t, 2, axis=-1)
            t2 = jnp.pad(t2, ((0, 0), (1, 0), (0, 0)))[:, :-1]
            return jnp.concatenate([t1, t2], axis=-1)

        def l2norm(t):
            return t / jnp.clip(jnp.linalg.norm(t, axis=-1, keepdims=True), 1e-12)

        def rotate_half(x):
            x1, x2 = jnp.split(x, 2, axis=-1)
            return jnp.concatenate([-x2, x1], axis=-1)

        def rotary_xpos(q, k):
            n = q.shape[-2]
            half_idx = jnp.arange(0, DIM_HEAD, 2, dtype=jnp.float32)
            inv_freq = 1.0 / 10000.0 ** (half_idx / DIM_HEAD)
            t = jnp.arange(n, dtype=jnp.float32)
            freqs = t[:, None] * inv_freq[None, :]
            freqs = jnp.concatenate([freqs, freqs], axis=-1)
            base = (half_idx + 0.4 * DIM_HEAD) / (1.4 * DIM_HEAD)
            power = (t - n // 2) / float(WINDOW // 2)
            scale = base[None, :] ** power[:, None]
            scale = jnp.concatenate([scale, scale], axis=-1)
            cos, sin = (jnp.cos(freqs), jnp.sin(freqs))
            q = q * cos * scale + rotate_half(q) * sin * scale
            k = k * cos / scale + rotate_half(k) * sin / scale
            return (q, k)

        def local_attention(q, k, v):
            b, h, n, d = q.shape
            w = n // WINDOW
            bq = q.reshape(b, h, w, WINDOW, d) * QK_SCALE
            bk = k.reshape(b, h, w, WINDOW, d)
            bv = v.reshape(b, h, w, WINDOW, d)

            def look_around(t):
                p = jnp.pad(t, ((0, 0), (0, 0), (1, 0), (0, 0), (0, 0)))
                return jnp.concatenate([p[:, :, :w], p[:, :, 1:]], axis=3)
            bk, bv = (look_around(bk), look_around(bv))
            bt = jnp.arange(n).reshape(w, WINDOW)
            btp = jnp.pad(bt, ((1, 0), (0, 0)), constant_values=-1)
            btk = jnp.concatenate([btp[:w], btp[1:]], axis=1)
            sim = jnp.einsum('bhwid,bhwjd->bhwij', bq, bk)
            i = bt[:, :, None]
            j = btk[:, None, :]
            mask = (i < j) | (i > j + WINDOW) | (j == -1)
            sim = jnp.where(mask, -jnp.finfo(sim.dtype).max, sim)
            attn = jax.nn.softmax(sim, axis=-1)
            out = jnp.einsum('bhwij,bhwjd->bhwid', attn, bv)
            return out.reshape(b, h, n, d)

        def _layer(x, wqkv, qs, ksc, wo, lg, lb, w1, b1, w2, b2):
            b, n, _ = x.shape
            h = shift_token(x)
            qkv = h @ wqkv
            q, k, v = jnp.split(qkv, 3, axis=-1)
            to_heads = lambda t: t.reshape(b, n, HEADS, DIM_HEAD).transpose(0, 2, 1, 3)
            q, k, v = (to_heads(q), to_heads(k), to_heads(v))
            q = l2norm(q) * qs
            k = l2norm(k) * ksc
            q, k = rotary_xpos(q, k)
            o = local_attention(q, k, v)
            o = o.transpose(0, 2, 1, 3).reshape(b, n, INNER)
            x = x + o @ wo
            h = shift_token(x)
            mu = h.mean(-1, keepdims=True)
            var = h.var(-1, keepdims=True)
            h = (h - mu) / jnp.sqrt(var + 1e-05) * lg + lb
            h = h @ w1 + b1
            a, g = jnp.split(h, 2, axis=-1)
            h = a * jax.nn.gelu(g, approximate=False)
            x = x + h @ w2 + b2
            return x
        for l in range(DEPTH):
            x = _layer(x, wqkv[l], q_scale[l], k_scale[l], wo[l], ln_g[l], ln_b[l], w1[l], b1[l], w2[l], b2[l])
        return x
    x = L0_attn_x
    x = x + _layernorm(_L0_attn_ref(_layernorm(x, axis=-1), L0_attn_W, L0_attn_b), axis=-1)
    x = x + _layernorm(_L0_ffn_ref(_layernorm(x, axis=-1), L0_ffn_wqkv, L0_ffn_q_scale, L0_ffn_k_scale, L0_ffn_wo, L0_ffn_ln_g, L0_ffn_ln_b, L0_ffn_w1, L0_ffn_b1, L0_ffn_w2, L0_ffn_b2), axis=-1)
    return x

_drawn_inputs = setup_inputs


def setup_inputs(seed=0):
    import zlib

    import numpy as np

    out = dict(_drawn_inputs(seed))
    spreads = {'L0_attn_b': (0.0, 0.1),
     'L0_ffn_q_scale': (1.0, 0.6),
     'L0_ffn_k_scale': (1.0, 0.6),
     'L0_ffn_ln_g': (1.0, 0.6),
     'L0_ffn_ln_b': (0.0, 0.8),
     'L0_ffn_b1': (0.0, 0.8),
     'L0_ffn_b2': (0.0, 0.8)}
    factors = {'L0_ffn_w1': 7.745, 'L0_ffn_w2': 7.671}
    for name, (base, spread) in spreads.items():
        noise = np.random.default_rng([zlib.crc32(name.encode()), seed]).standard_normal(out[name].shape)
        drawn = base * np.exp(spread * noise) if base else spread * noise
        out[name] = jnp.asarray(drawn.astype(out[name].dtype))
    for name, factor in factors.items():
        out[name] = (out[name] * factor).astype(out[name].dtype)
    return out
```

```python
import concourse.bass as bass
from concourse import mybir
from contextlib import ExitStack

P = 128
BATCH = 8
SEQ = 1024
DIM = 128
TPB = SEQ // P
TILES = BATCH * TPB
DEPTH = 2
HEADS = 8
DH = 64
INNER = HEADS * DH
WINDOW = 64
HALF = DH // 2
HID = int(DIM * 4 * 2 / 3)
HBLK = [(0, P), (P, P), (2 * P, HID - 2 * P)]
NB = len(HBLK)
TAIL = HBLK[-1][1]
GT = 4
GROUPS = TILES // GT
BANK = 512
LN_EPS = 1e-5
NORM_MIN2 = 1e-24
ATT_SCALE = float(DIM) ** -0.5
QK_SCALE = 8.0
NEG = -3.0e38
DMA = 16


def build_program(nc, x, W, b, wqkv, q_scale, k_scale, wo, ln_g, ln_b, w1, b1, w2, b2, xpos, out):
    f32, bf16 = mybir.dt.float32, mybir.dt.bfloat16
    ALU, ACT, AX = mybir.AluOpType, mybir.ActivationFunctionType, mybir.AxisListType
    mm, tr = nc.tensor.matmul, nc.tensor.transpose

    with ExitStack() as ctx:
        def sb(name, shape, dt=f32):
            return ctx.enter_context(nc.sbuf_tensor(name, shape, dt))

        def sem(name):
            return ctx.enter_context(nc.semaphore(name))

        xs = sb("xs", [P, TILES, DIM])
        ys = sb("ys", [P, BATCH * (TPB + 1), DIM])
        ident = sb("ident", [P, P])
        identb = sb("identb", [P, P], bf16)
        causal = sb("causal", [P, P], bf16)
        band = sb("band", [P, 2, BANK], bf16)
        carrier = sb("carrier", [P, 1])
        eps = sb("eps", [P, TPB])
        half_neg = sb("half_neg", [P, 2 * HEADS])
        w_in = sb("w_in", [P, 3 * DIM])
        b_col = sb("b_col", [P, 2])
        bv_all = sb("bv_all", [P, DIM])
        region = sb("region", [P, 16896])
        used = [0]

        def part(*shape):
            n = 1
            for s in shape:
                n *= s
            v = region[:, used[0]:used[0] + n]
            used[0] += n
            assert used[0] <= 16896, used[0]
            if len(shape) == 2:
                v = v.rearrange("p (a b) -> p a b", a=shape[0])
            if len(shape) == 3:
                v = v.rearrange("p (a b c) -> p a b c", a=shape[0], b=shape[1])
            return v

        st = sb("st", [P, TPB, 6])
        mv = sb("mv", [P, TPB, 2])
        rstd = sb("rstd", [P, TPB])

        xn = part(TPB, DIM)
        xT = part(SEQ)
        qT = part(SEQ)
        kT = part(SEQ)
        v_sb = part(TPB, DIM)
        prob = part(2, SEQ)
        pT = part(SEQ)
        o_sb = part(TPB, DIM)
        negmax = sb("negmax", [P, 2])
        rowsum = sb("rowsum", [P, 2])
        rinv = sb("rinv", [P, 2])

        used[0] = 0
        w_qkv = sb("w_qkv", [P, 3 * INNER])
        w_o = sb("w_o", [P, INNER // P, DIM])
        base = sb("base", [P, TPB, 4, DH])
        tab = sb("tab", [P, TPB, 4, DH])
        qks = sb("qks", [P, 4, DH])
        h_in = part(2, DIM)
        hT = part(P)
        sq = part(2 * INNER)
        termA = part(2 * INNER)
        termB = part(2 * INNER)
        rsum = part(2 * INNER)
        qk_rot = part(2 * INNER)
        wqT = part(HEADS // 2, P)
        wkT = part(2, HEADS // 2, P + WINDOW)
        wv = part(2, INNER)
        wvs = part(2, INNER)
        wprob = part(HEADS, P)
        wpT = part(HEADS, P)
        o_n = part(INNER)
        oT = part(HEADS // 2, P)
        ss = sb("ss", [P, 2 * HEADS])
        rr = sb("rr", [P, 2 * HEADS])
        wnegmax = sb("wnegmax", [P, HEADS])
        wrowsum = sb("wrowsum", [P, 2, HEADS])
        wrinv = sb("wrinv", [P, HEADS])

        used[0] = 0
        w_1 = sb("w_1", [P, 2 * HID])
        w_2 = sb("w_2", [P, NB, DIM])
        b_1 = sb("b_1", [P, 2, NB])
        ln_cols = sb("ln_cols", [P, 2])
        hc = part(2, GT, DIM)
        hcT = part(GT * P)
        gel = part(NB, GT * P)
        hid = part(2 * NB, GT * P)
        fst = sb("fst", [P, GT, 6])
        fmv = sb("fmv", [P, GT, 2])
        frs = sb("frs", [P, GT])
        used[0] = 0
        res = part(2, TPB, DIM)

        PS = ctx.enter_context(nc.psum_tensor("PS", [P, 8 * BANK], f32))

        def bank(n, cols=BANK, off=0):
            return PS[:, n * BANK + off:n * BANK + off + cols]

        names = """consts iota0 w_in_ld wl_ld x_ld zeroed
            a_mv a_rstd a_xn a_xt_ps a_xt_a a_xt_v a_q_ps a_k_ps a_v_ps a_qT a_kT a_v
            a_sc a_nm a_exp a_pt a_pt_a a_pt_v a_pv a_o a_omv a_orstd a_x1 a_ymv a_yrstd a_bcol
            dve_step pool_step stream
            h_ld0 h_ld1 xt_ps h_t q_ps k_ps v_ps sq_ok ss_sum ss_ok rr_ok rot_terms rot_sum qk_ok tr_ps qk_t sc_ps nm_ok
            probs pt_ps pt_a pt_v v_ok vs_hi0 vs_hi1 vs_lo0 vs_lo1 o_ps o_ok ot_ps ot_ok wo_ps
            hc_ld0 hc_ld1 c_mv c_rs c_hn c_t_ps c_hT c_g_ps c_gel c_hid c_out_ps c_out_free
            d_mv d_rs d_nrm d_st0 d_st1 a_y a_rinv updated""".split()
        S = {n: sem(n) for n in names}

        def head(j):
            return 2 * (j % (HEADS // 2)) + j // (HEADS // 2)

        def h_loaded(l, t, u):
            return S[f"h_ld{u}"], 3 * DMA * (l * (TILES // 2) + (t >> 1) + 1)

        def hi_shifted(l, t, u):
            return S[f"vs_hi{u}"], DMA * (l * (TILES // 2) + (t >> 1) + 1)

        def lo_shifted(l, t, u):
            return S[f"vs_lo{u}"], DMA * (l * (TILES // 2 - u) + (t >> 1) + 1)

        def group_loaded(l, g, u):
            return S[f"hc_ld{u}"], 3 * DMA * (l * (GROUPS // 2) + (g >> 1) + 1)

        def bounded(v, low, high):
            return v.with_bounds(min_val=low, max_val=high)

        def yslot(t):
            if isinstance(t, int):
                return t + t // TPB + 1
            return bounded(t + (t >> 3) + 1, 1, BATCH * (TPB + 1) - 1)

        block = ctx.enter_context(nc.Block())
        x_t = x.rearrange("b (i p) c -> b p i c", p=P)
        out_t = out.rearrange("b (i p) c -> b p i c", p=P)

        @block.sync
        def _(sp):
            sp.dma_start(w_in[:], W).then_inc(S["w_in_ld"], DMA)
            sp.dma_start(b_col[:], b[0:2 * DIM].rearrange("(s c) -> c s", s=2),
                         allow_slow_non_contiguous=True).then_inc(S["w_in_ld"], DMA)
            sp.dma_start(bv_all[:], b[2 * DIM:3 * DIM].partition_broadcast(P)).then_inc(S["w_in_ld"], DMA)
            for n in range(BATCH):
                if n:
                    sp.wait_ge(S["x_ld"], DMA * n)
                sp.dma_start(xs[:, n * TPB:(n + 1) * TPB, :], x_t[n]).then_inc(S["x_ld"], DMA)
            sp.dma_start(base[:], xpos).then_inc(S["consts"], DMA)

            def shifted(l, t, u, free=None):
                s = sp.snap(yslot(t)) if free is not None else yslot(t)
                if free is not None:
                    sp.wait_ge(S["xt_ps"], free)
                sp.dma_start(h_in[:, u, 0:DIM // 2], ys[:, bass.ds(s, 1), 0:DIM // 2]).then_inc(S[f"h_ld{u}"], DMA)
                sp.dma_start(h_in[1:P, u, DIM // 2:], ys[0:P - 1, bass.ds(s, 1), DIM // 2:]).then_inc(S[f"h_ld{u}"], DMA)
                sp.dma_start(h_in[0:1, u, DIM // 2:], ys[P - 1:P, bass.ds(s - 1, 1), DIM // 2:]).then_inc(S[f"h_ld{u}"], DMA)

            def v_shift(l, t, u, first, last):
                G = l * TILES + t
                sp.wait_ge(S["v_ok"], G + 1)
                sp.dma_start(wvs[WINDOW:P, u, :], wv[0:WINDOW, u, :]).then_inc(S[f"vs_hi{u}"], DMA)
                if not last:
                    if not first:
                        sp.wait_ge(S["o_ps"], G)
                    sp.dma_start(wvs[0:WINDOW, 1 - u, :], wv[WINDOW:P, u, :]).then_inc(S[f"vs_lo{u}"], DMA)

            def shifted_group(l, bt, gu):
                s = bt * (TPB + 1) + 1 + gu * GT
                sp.dma_start(hc[:, gu, :, 0:DIM // 2], ys[:, bass.ds(s, GT), 0:DIM // 2]).then_inc(S[f"hc_ld{gu}"], DMA)
                sp.dma_start(hc[1:P, gu, :, DIM // 2:], ys[0:P - 1, bass.ds(s, GT), DIM // 2:]).then_inc(S[f"hc_ld{gu}"], DMA)
                sp.dma_start(hc[0:1, gu, :, DIM // 2:], ys[P - 1:P, bass.ds(s - 1, GT), DIM // 2:]).then_inc(S[f"hc_ld{gu}"], DMA)

            with sp.Fori(0, DEPTH) as l:
                sp.wait_ge(S["stream"], 2 * l + 1)
                loads = [
                    (w_qkv[:], wqkv[bass.ds(l, 1)].rearrange("a c n -> (a c) n")),
                    (w_o[:], wo[bass.ds(l, 1)].rearrange("a (k c) n -> (a c) k n", c=P)),
                    (w_1[:], w1[bass.ds(l, 1)].rearrange("a c n -> (a c) n")),
                    (w_2[:, 0:2, :], w2[bass.ds(l, 1), 0:2 * P].rearrange("a (k c) n -> (a c) k n", c=P)),
                    (w_2[0:TAIL, 2, :], w2[bass.ds(l, 1), 2 * P:HID].rearrange("a c n -> (a c) n")),
                    (w_2[TAIL:TAIL + 1, 2, :], b2[bass.ds(l, 1)]),
                    (ln_cols[:, 0:1], ln_g[bass.ds(l, 1)].rearrange("a c -> c a")),
                    (ln_cols[:, 1:2], ln_b[bass.ds(l, 1)].rearrange("a c -> c a")),
                    (qks[:, 0, :], q_scale[bass.ds(l, 1)].rearrange("a c -> (a c)").partition_broadcast(P)),
                    (qks[:, 1, :], k_scale[bass.ds(l, 1)].rearrange("a c -> (a c)").partition_broadcast(P)),
                ]
                for s, scale in ((2, q_scale), (3, k_scale)):
                    for h in range(2):
                        loads.append((qks[:, s, h * HALF:(h + 1) * HALF],
                                      scale[bass.ds(l, 1), (1 - h) * HALF:(2 - h) * HALF]
                                      .rearrange("a c -> (a c)").partition_broadcast(P)))
                for s in range(2):
                    for m, (o, n) in enumerate(HBLK):
                        loads.append((b_1[0:n, s, m:m + 1],
                                      b1[bass.ds(l, 1), s * HID + o:s * HID + o + n].rearrange("a c -> c a")))
                for dst, src in loads:
                    sp.dma_start(dst, src, allow_slow_non_contiguous=True).then_inc(S["wl_ld"], DMA)

                shifted(l, 0, 0)
                shifted(l, 1, 1)
                v_shift(l, 0, 0, True, False)
                with sp.Fori(0, TILES // 2 - 1) as p:
                    for k in (1, 2):
                        t, u = 2 * p + k, k % 2
                        shifted(l, t + 1, 1 - u, l * TILES + t)
                        v_shift(l, t, u, False, False)
                v_shift(l, TILES - 1, 1, False, True)

                sp.wait_ge(S["stream"], 2 * l + 2)
                shifted_group(l, 0, 0)
                shifted_group(l, 0, 1)
                with sp.Fori(1, BATCH) as bt:
                    for gu in range(2):
                        sp.wait_ge(S["c_t_ps"], l * GROUPS + 2 * bt + gu - 1)
                        shifted_group(l, bt, gu)

            for n in range(BATCH):
                sp.wait_ge(S["d_nrm"], n + 1)
                sp.dma_start(out_t[n], res[:, n % 2]).then_inc(S[f"d_st{n % 2}"], DMA)
            for u in range(2):
                sp.wait_ge(S[f"d_st{u}"], DMA * BATCH // 2)

        @block.gpsimd
        def _(pool):
            pool.memset(ident[:], 0.0).then_inc(S["iota0"], 1)
            pool.memset(causal[:], 0.0).then_inc(S["iota0"], 1)
            pool.memset(band[:], 0.0).then_inc(S["iota0"], 1)
            pool.memset(half_neg[:], -0.5)
            pool.memset(eps[:], LN_EPS).then_inc(S["zeroed"], 1)
            pool.memset(ys[:, :, :].rearrange("p (n i) c -> p n i c", n=BATCH)[:, :, 0, :], 0.0).then_inc(S["zeroed"], 1)
            pool.wait_ge(S["iota0"], 3)
            pool.affine_select(out=ident[:], in_=ident[:], compare_op=ALU.not_equal, fill=1.0, base=0,
                               pattern=[[-1, P]], channel_multiplier=1).then_inc(S["iota0"], 1)
            pool.affine_select(out=causal[:], in_=causal[:], compare_op=ALU.is_ge, fill=NEG, base=0,
                               pattern=[[-1, P]], channel_multiplier=1).then_inc(S["zeroed"], 1)
            n = 4
            for lo in (0, WINDOW):
                rows = band[lo:lo + WINDOW].rearrange("p s (h c) -> p (s h) c", c=P)
                pool.wait_ge(S["iota0"], n)
                pool.affine_select(out=rows, in_=rows, compare_op=ALU.is_ge, fill=NEG, base=0,
                                   pattern=[[0, 2 * BANK // P], [1, P]], channel_multiplier=-1).then_inc(S["iota0"], 1)
                n += 1
                pool.wait_ge(S["iota0"], n)
                pool.affine_select(out=rows, in_=rows, compare_op=ALU.is_ge, fill=NEG, base=WINDOW,
                                   pattern=[[0, 2 * BANK // P], [-1, P]], channel_multiplier=1).then_inc(S["iota0"], 1)
                n += 1
            pool.wait_ge(S["iota0"], n)
            pool.memset(band[0:WINDOW, 0, :].rearrange("p (h c) -> p h c", c=P)[:, :, 0:WINDOW], NEG).then_inc(S["zeroed"], 1)

            def rsqrt(dst, src, wait, done, n):
                pool.wait_ge(S[wait[0]], wait[1])
                pool.tensor_tensor(dst, src, eps[:, 0:n], ALU.add).then_inc(S["pool_step"], 1)
                pool.wait_ge(S["pool_step"], pstep(1))
                pool.tensor_tensor(dst, dst, half_neg[:, 0:n], ALU.pow).then_inc(S[done], 1)

            def pstep(k):
                return pcount[0] + k
            pcount = [0]
            pool.wait_ge(S["zeroed"], 5)

            with pool.Fori(0, BATCH) as bt:
                for i, (src, dst, wait, done) in enumerate([(mv, rstd, "a_mv", "a_rstd"), (mv, rstd, "a_omv", "a_orstd"),
                                                            (mv, rstd, "a_ymv", "a_yrstd")]):
                    pcount[0] = bt * 3 + i
                    rsqrt(dst[:], src[:, :, 1], (wait, bt + 1), done, TPB)

            with pool.Fori(0, DEPTH) as l:
                def norms(t, first):
                    G = l * TILES + t
                    pool.wait_ge(S["ss_ok"], G + 1)
                    if not first:
                        pool.wait_ge(S["qk_ok"], G)
                    pool.tensor_tensor(rr[:], ss[:], half_neg[:], ALU.pow).then_inc(S["rr_ok"], 1)
                    pool.wait_ge(S["rot_terms"], G + 1)
                    pool.tensor_tensor(rsum[:], termA[:], termB[:], ALU.add).then_inc(S["rot_sum"], 1)

                norms(0, True)
                with pool.Fori(0, TILES // 2 - 1) as p:
                    norms(2 * p + 1, False)
                    norms(2 * p + 2, False)
                norms(TILES - 1, False)
                with pool.Fori(0, GROUPS) as g:
                    pcount[0] = 3 * BATCH + l * GROUPS + g
                    rsqrt(frs[:], fmv[:, :, 1], ("c_mv", l * GROUPS + g + 1), "c_rs", GT)

            for n in range(BATCH):
                pcount[0] = 3 * BATCH + DEPTH * GROUPS + n
                rsqrt(rstd[:], mv[:, :, 1], ("d_mv", n + 1), "d_rs", TPB)

        @block.scalar
        def _(act):
            A = act.activation
            act.wait_ge(S["a_bcol"], 1)
            with act.Fori(0, BATCH) as bt:
                act.wait_ge(S["a_xt_ps"], 2 * bt + 1)
                A(xT[:, 0:BANK], bank(0), ACT.Copy).then_inc(S["a_xt_a"], 1)
                for j in range(2):
                    act.wait_ge(S["a_q_ps"], 2 * bt + j + 1)
                    A(qT[:, j * BANK:(j + 1) * BANK], bank(2 + j), ACT.Identity, bias=b_col[:, 0:1],
                      scale=ATT_SCALE).then_inc(S["a_qT"], 1)

                def exps(i):
                    n = (i + 1) * P
                    act.wait_ge(S["a_nm"], bt * TPB + i + 1)
                    A(prob[:, i % 2, 0:n], PS[:, (i % 2) * 2 * BANK:(i % 2) * 2 * BANK + n], ACT.Exp,
                      bias=negmax[:, i % 2:i % 2 + 1], accum_out=rowsum[:, i % 2:i % 2 + 1]).then_inc(S["a_exp"], 1)

                exps(0)
                for i in range(TPB):
                    if i + 1 < TPB:
                        exps(i + 1)
                    act.wait_ge(S["a_pt"], bt * TPB + i + 1)
                    n = min((i + 1) * P, BANK)
                    A(pT[:, 0:n], bank(4, n), ACT.Copy).then_inc(S["a_pt_a"], 1)

            with act.Fori(0, DEPTH) as l:
                act.wait_ge(S["stream"], 2 * l + 1)

                def h_evac(t):
                    act.wait_ge(S["xt_ps"], l * TILES + t + 1)
                    A(hT, bank(2, P), ACT.Copy).then_inc(S["h_t"], 1)

                def squares(t, first):
                    G = l * TILES + t
                    if not first:
                        act.wait_ge(S["ss_ok"], G)
                    for s, ps in enumerate(("q_ps", "k_ps")):
                        act.wait_ge(S[ps], G + 1)
                        A(sq[:, s * INNER:(s + 1) * INNER], bank(s), ACT.Square).then_inc(S["sq_ok"], 1)

                def v_evac(t, u, early):
                    G = l * TILES + t
                    act.wait_ge(S["v_ps"], G + 1)
                    if not early:
                        act.wait_ge(S["o_ps"], G - 1)
                        act.wait_ge(*hi_shifted(l, t - 2, u))
                        act.wait_ge(*lo_shifted(l, t - 2, u))
                    A(wv[:, u, :], bank(2), ACT.Copy).then_inc(S["v_ok"], 1)

                def exps(t, u, half):
                    G = l * TILES + t
                    act.wait_ge(S["nm_ok"], 2 * G + half + 1)
                    for j in range(half * 4, half * 4 + 4):
                        last = A(wprob[:, j, :], bank(3 + half, P, (j % 4) * P), ACT.Exp,
                                 bias=wnegmax[:, j:j + 1], accum_out=wrowsum[:, u, head(j):head(j) + 1])
                    last.then_inc(S["probs"], 1)

                def qk_evac(t, u):
                    act.wait_ge(S["tr_ps"], l * TILES + t + 1)
                    A(wqT, bank(5), ACT.Copy)
                    kps = bank(6).rearrange("p (g c) -> p g c", c=P)
                    A(wkT[:, u, :, WINDOW:], kps, ACT.Copy)
                    A(wkT[:, 1 - u, :, 0:WINDOW], kps[:, :, P - WINDOW:], ACT.Copy).then_inc(S["qk_t"], 1)

                def pt_evac(t):
                    act.wait_ge(S["pt_ps"], 2 * (l * TILES + t) + 1)
                    A(wpT[:, 0:4, :], bank(3), ACT.Copy).then_inc(S["pt_a"], 1)

                def ot_evac(t):
                    act.wait_ge(S["ot_ps"], l * TILES + t + 1)
                    A(oT, bank(5), ACT.Copy).then_inc(S["ot_ok"], 1)

                def slot(t, u, first=False, second=False, last=False, end=False):
                    if not first:
                        exps(t - 1, 1 - u, 0)
                    if not (last or end):
                        h_evac(t + 1)
                    if not first:
                        exps(t - 1, 1 - u, 1)
                    if not (last or end):
                        squares(t + 1, False)
                    if not first:
                        pt_evac(t - 1)
                    if not end:
                        qk_evac(t, u)
                    if not (last or end):
                        v_evac(t + 1, 1 - u, first)
                    if not first:
                        ot_evac(t - 1)

                h_evac(0)
                squares(0, True)
                v_evac(0, 0, True)
                slot(0, 0, first=True)
                with act.Fori(0, TILES // 2 - 1) as p:
                    slot(2 * p + 1, 1)
                    slot(2 * p + 2, 0)
                slot(TILES - 1, 1, last=True)
                slot(TILES, 0, end=True)

                act.wait_ge(S["stream"], 2 * l + 2)

                def hT_evac(g):
                    act.wait_ge(S["c_t_ps"], l * GROUPS + g + 1)
                    A(hcT, bank(2), ACT.Identity, bias=ln_cols[:, 1:2], scale=ln_cols[:, 0:1]).then_inc(S["c_hT"], 1)

                def gelus(g):
                    for m, (o, n) in enumerate(HBLK):
                        act.wait_ge(S["c_g_ps"], NB * (l * GROUPS + g) + m + 1)
                        A(gel[0:n, m, :], bank(5 + m)[0:n], ACT.Gelu, bias=b_1[0:n, 1, m:m + 1]).then_inc(S["c_gel"], 1)

                hT_evac(0)
                with act.Fori(0, GROUPS - 1) as g:
                    gelus(g)
                    hT_evac(g + 1)
                gelus(GROUPS - 1)

        @block.vector
        def _(dve):
            V = nc.vector

            def wait_then_go(semaphore, value):
                dve.wait_ge(semaphore, value)
                V.memset(carrier[:], 0.0)

            def stats(dst_mv, dst_st, tiles, n, base_count, s="dve_step"):
                for i in range(n):
                    last = V.bn_stats(dst_st[:, i, :], tiles(i))
                last.then_inc(S[s], 1)
                wait_then_go(S[s], base_count + 1)
                for i in range(n):
                    last = V.bn_aggr(dst_mv[:, i, :], dst_st[:, i, :])
                return last

            dve.sem_inc(S["c_out_free"], 2)
            dve.wait_ge(S["w_in_ld"], 3 * DMA)
            V.tensor_scalar(b_col[:, 0:1], b_col[:, 0:1], ATT_SCALE, None, ALU.mult).then_inc(S["a_bcol"], 1)
            dve.wait_ge(S["iota0"], 4)
            V.tensor_copy(identb[:], ident[:]).then_inc(S["zeroed"], 1)
            dve.wait_ge(S["zeroed"], 5)
            with dve.Fori(0, BATCH) as bt:
                K = 3 * bt
                wait_then_go(S["x_ld"], DMA * (bt + 1))
                at = lambda i: xs[:, bass.ds(bt * TPB + i, 1), :].rearrange("p a c -> p (a c)")
                yt = lambda i: ys[:, bass.ds(bt * (TPB + 1) + 1 + i, 1), :].rearrange("p a c -> p (a c)")
                stats(mv, st, at, TPB, K).then_inc(S["a_mv"], 1)
                dve.wait_ge(S["a_rstd"], bt + 1)
                for i in range(TPB):
                    last = V.tensor_scalar(xn[:, i, :], at(i), mv[:, i, 0:1], rstd[:, i:i + 1], ALU.subtract, ALU.mult)
                last.then_inc(S["a_xn"], 1)
                dve.wait_ge(S["a_xt_ps"], 2 * bt + 2)
                V.tensor_copy(xT[:, BANK:], bank(1)).then_inc(S["a_xt_v"], 1)
                for j in range(2):
                    dve.wait_ge(S["a_k_ps"], 2 * bt + j + 1)
                    V.tensor_scalar(kT[:, j * BANK:(j + 1) * BANK], bank(4 + j), b_col[:, 1:2], None,
                                    ALU.add).then_inc(S["a_kT"], 1)
                for j in range(2):
                    dve.wait_ge(S["a_v_ps"], 2 * bt + j + 1)
                    V.tensor_tensor(v_sb[:, 4 * j:4 * j + 4, :], bank(6 + j).rearrange("p (i c) -> p i c", c=DIM),
                                    bv_all[:].unsqueeze(1).broadcast_to([P, 4, DIM]), ALU.add).then_inc(S["a_v"], 1)

                def rowmax(i):
                    dve.wait_ge(S["a_sc"], bt * TPB + i + 1)
                    V.tensor_reduce(negmax[:, i % 2:i % 2 + 1],
                                    PS[:, (i % 2) * 2 * BANK:(i % 2) * 2 * BANK + (i + 1) * P], AX.X, ALU.max,
                                    negate=True).then_inc(S["a_nm"], 1)

                rowmax(0)
                for i in range(TPB):
                    if i + 1 < TPB:
                        rowmax(i + 1)
                    dve.wait_ge(S["a_exp"], bt * TPB + i + 1)
                    V.reciprocal(rinv[:, i % 2:i % 2 + 1], rowsum[:, i % 2:i % 2 + 1]).then_inc(S["a_rinv"], 1)
                    if i >= 4:
                        dve.wait_ge(S["a_pt"], bt * TPB + i + 1)
                        V.tensor_copy(pT[:, BANK:(i + 1) * P], bank(5, (i + 1) * P - BANK)).then_inc(S["a_pt_v"], 1)
                    dve.wait_ge(S["a_pv"], bt * TPB + i + 1)
                    dve.wait_ge(S["a_rinv"], bt * TPB + i + 1)
                    V.tensor_scalar(o_sb[:, i, :], bank(6 + i % 2, DIM), rinv[:, i % 2:i % 2 + 1], None,
                                    ALU.mult).then_inc(S["a_o"], 1)
                wait_then_go(S["a_o"], (bt + 1) * TPB)
                stats(mv, st, lambda i: o_sb[:, i, :], TPB, K + 1).then_inc(S["a_omv"], 1)
                dve.wait_ge(S["a_orstd"], bt + 1)
                for i in range(TPB):
                    last = V.tensor_scalar(o_sb[:, i, :], o_sb[:, i, :], mv[:, i, 0:1], rstd[:, i:i + 1],
                                           ALU.subtract, ALU.mult)
                last.then_inc(S["a_x1"], 1)
                dve.wait_ge(S["a_x1"], 2 * bt + 1)
                xb = xs[:, bass.ds(bt * TPB, TPB), :]
                V.tensor_tensor(xb, xb, o_sb, ALU.add).then_inc(S["a_x1"], 1)
                wait_then_go(S["a_x1"], 2 * bt + 2)
                stats(mv, st, at, TPB, K + 2).then_inc(S["a_ymv"], 1)
                dve.wait_ge(S["a_yrstd"], bt + 1)
                for i in range(TPB):
                    last = V.tensor_scalar(yt(i), at(i), mv[:, i, 0:1], rstd[:, i:i + 1], ALU.subtract, ALU.mult)
                last.then_inc(S["a_y"], 1)
            dve.wait_ge(S["a_y"], BATCH)
            V.memset(wkT[:, 0, :, 0:WINDOW], 0.0).then_inc(S["dve_step"], 1)
            V.memset(wvs[0:WINDOW, 0, :], 0.0).then_inc(S["dve_step"], 1)
            dve.wait_ge(S["dve_step"], 3 * BATCH + 2)
            dve.sem_inc(S["stream"], 1)
            D0 = 3 * BATCH + 2
            PER = 1 + 1 + TILES + GROUPS
            with dve.Fori(0, DEPTH) as l:
                L0 = D0 + l * PER
                dve.wait_ge(S["consts"], DMA)
                dve.wait_ge(S["wl_ld"], DMA * 20 * (l + 1))
                V.tensor_tensor(tab[:], base[:], qks[:].unsqueeze(1).broadcast_to([P, TPB, 4, DH]),
                                ALU.mult).then_inc(S["dve_step"], 1)
                dve.wait_ge(S["dve_step"], L0 + 1)

                def sumsq(t):
                    G = l * TILES + t
                    dve.wait_ge(S["sq_ok"], 2 * G + 2)
                    V.tensor_reduce(ss[:], sq.rearrange("p (h d) -> p h d", d=DH), AX.X, ALU.add).then_inc(S["ss_sum"], 1)
                    dve.wait_ge(S["ss_sum"], G + 1)
                    V.tensor_scalar(ss[:], ss[:], NORM_MIN2, None, ALU.max).then_inc(S["ss_ok"], 1)

                def rotate(t, first):
                    G = l * TILES + t
                    if not first:
                        dve.wait_ge(S["rot_sum"], G)
                    i = (t & (TPB - 1)) if not isinstance(t, int) else t % TPB
                    def split(a):
                        return a.rearrange("p (s h d) -> p s h d", s=2, d=DH)
                    tb = tab[:, bass.ds(i, 1), :, :].rearrange("p a s d -> p (a s) d")
                    qk = PS[:, 0:2 * BANK]
                    V.tensor_tensor(split(termA), split(qk), tb[:, 0:2, :].unsqueeze(2).broadcast_to([P, 2, HEADS, DH]), ALU.mult)
                    for h in range(2):
                        o, f = h * HALF, (1 - h) * HALF
                        last = V.tensor_tensor(split(termB)[:, :, :, o:o + HALF], split(qk)[:, :, :, f:f + HALF],
                                               tb[:, 2:4, o:o + HALF].unsqueeze(2).broadcast_to([P, 2, HEADS, HALF]), ALU.mult)
                    last.then_inc(S["rot_terms"], 1)

                def normalize(t, first):
                    G = l * TILES + t
                    dve.wait_ge(S["rot_sum"], G + 1)
                    dve.wait_ge(S["rr_ok"], G + 1)
                    if not first:
                        dve.wait_ge(S["tr_ps"], G)
                    V.tensor_tensor(qk_rot.rearrange("p (h d) -> p h d", d=DH), rsum.rearrange("p (h d) -> p h d", d=DH),
                                    rr[:].unsqueeze(2).broadcast_to([P, 2 * HEADS, DH]), ALU.mult).then_inc(S["qk_ok"], 1)

                def rowmax(t):
                    G = l * TILES + t
                    for half in range(2):
                        dve.wait_ge(S["sc_ps"], 2 * G + half + 1)
                        V.tensor_reduce(wnegmax[:, 4 * half:4 * half + 4], bank(3 + half).rearrange("p (h c) -> p h c", c=P),
                                        AX.X, ALU.max, negate=True).then_inc(S["nm_ok"], 1)

                def pt_evac(t):
                    dve.wait_ge(S["pt_ps"], 2 * (l * TILES + t) + 2)
                    V.tensor_copy(wpT[:, 4:8, :], bank(4).rearrange("p (h c) -> p h c", c=P)).then_inc(S["pt_v"], 1)

                def o_norm(t, u):
                    G = l * TILES + t
                    dve.wait_ge(S["probs"], 2 * G + 2)
                    V.reciprocal(wrinv[:], wrowsum[:, u, :]).then_inc(S["dve_step"], 1)
                    dve.wait_ge(S["dve_step"], L0 + 1 + t + 1)
                    dve.wait_ge(S["o_ps"], G + 1)
                    V.tensor_tensor(o_n.rearrange("p (h d) -> p h d", d=DH), bank(7).rearrange("p (h d) -> p h d", d=DH),
                                    wrinv[:].unsqueeze(2).broadcast_to([P, HEADS, DH]), ALU.mult).then_inc(S["o_ok"], 1)

                def residual(t, u, end):
                    G = l * TILES + t
                    dve.wait_ge(S["wo_ps"], G + 1)
                    if not end:
                        dve.wait_ge(*h_loaded(l, t + 1, 1 - u))
                    yt = ys[:, bass.ds(yslot(t), 1), :].rearrange("p a c -> p (a c)")
                    V.tensor_tensor(yt, yt, bank(7, DIM), ALU.add).then_inc(S["updated"], 1)

                def slot(t, u, first=False, last=False, end=False):
                    if not first:
                        pt_evac(t - 1)
                    if not (last or end):
                        sumsq(t + 1)
                        rotate(t + 1, False)
                    if not first:
                        o_norm(t - 1, 1 - u)
                    if not (last or end):
                        normalize(t + 1, False)
                    if not end:
                        rowmax(t)
                    if not first:
                        residual(t - 1, 1 - u, end)

                sumsq(0)
                rotate(0, True)
                normalize(0, True)
                slot(0, 0, first=True)
                with dve.Fori(0, TILES // 2 - 1) as p:
                    slot(2 * p + 1, 1)
                    slot(2 * p + 2, 0)
                slot(TILES - 1, 1, last=True)
                slot(TILES, 0, end=True)
                dve.wait_ge(S["updated"], (l + 1) * TILES)
                for gu in range(2):
                    last = V.memset(hid[64:P, gu * NB + NB - 1, :], 1.0)
                last.then_inc(S["dve_step"], 1)
                dve.wait_ge(S["dve_step"], L0 + 1 + TILES + 1)
                dve.sem_inc(S["stream"], 1)

                C0 = L0 + 1 + TILES + 1

                def group_stats(g, gu):
                    wait_then_go(*group_loaded(l, g, gu))
                    stats(fmv, fst, lambda i: hc[:, gu, i, :], GT, C0 + g).then_inc(S["c_mv"], 1)

                def group_norm(g, gu):
                    dve.wait_ge(S["c_rs"], l * GROUPS + g + 1)
                    for i in range(GT):
                        last = V.tensor_scalar(hc[:, gu, i, :], hc[:, gu, i, :], fmv[:, i, 0:1], frs[:, i:i + 1],
                                               ALU.subtract, ALU.mult)
                    last.then_inc(S["c_hn"], 1)

                def gate(g, gu, m):
                    o, n = HBLK[m]
                    dve.wait_ge(S["c_gel"], NB * (l * GROUPS + g) + m + 1)
                    V.scalar_tensor_tensor(out=hid[0:n, gu * NB + m, :], in0=bank(2 + m)[0:n], scalar=b_1[0:n, 0, m:m + 1],
                                           in1=gel[0:n, m, :], op0=ALU.add, op1=ALU.mult).then_inc(S["c_hid"], 1)

                def group_residual(g, gu, end=False):
                    G = l * GROUPS + g
                    dve.wait_ge(S["c_out_ps"], G + 1)
                    if not end:
                        dve.wait_ge(*group_loaded(l, g + 1, 1 - gu))
                    s = (g >> 1) * (TPB + 1) + 1 + gu * GT
                    if not isinstance(g, int):
                        s = bounded(s, 1, BATCH * (TPB + 1) - GT)
                    yg = ys[:, bass.ds(s, GT), :]
                    V.tensor_tensor(yg, yg, bank(gu).rearrange("p (i c) -> p i c", c=DIM), ALU.add).then_inc(S["c_out_free"], 1)

                def gslot(g, gu, first=False, last=False):
                    if not last:
                        group_stats(g + 1, 1 - gu)
                    gate(g, gu, 0)
                    if not last:
                        group_norm(g + 1, 1 - gu)
                    gate(g, gu, 1)
                    gate(g, gu, 2)
                    if not first:
                        group_residual(g - 1, 1 - gu)

                group_stats(0, 0)
                group_norm(0, 0)
                gslot(0, 0, first=True)
                with dve.Fori(0, GROUPS // 2 - 1) as p:
                    gslot(2 * p + 1, 1)
                    gslot(2 * p + 2, 0)
                gslot(GROUPS - 1, 1, last=True)
                group_residual(GROUPS - 1, 1, end=True)
                dve.wait_ge(S["c_out_free"], 2 + (l + 1) * GROUPS)
                dve.sem_inc(S["stream"], 1)

            E0 = D0 + DEPTH * PER
            for n in range(BATCH):
                yv = lambda i: ys[:, n * (TPB + 1) + 1 + i, :]
                stats(mv, st, yv, TPB, E0 + 2 * n).then_inc(S["d_mv"], 1)
                dve.wait_ge(S["d_rs"], n + 1)
                if n >= 2:
                    dve.wait_ge(S[f"d_st{n % 2}"], DMA * (n // 2))
                for i in range(TPB):
                    last = V.tensor_scalar(res[:, n % 2, i, :], yv(i), mv[:, i, 0:1], rstd[:, i:i + 1],
                                           ALU.subtract, ALU.mult)
                last.then_inc(S["dve_step"], 1)
                dve.wait_ge(S["dve_step"], E0 + 2 * n + 2)
                V.tensor_tensor(res[:, n % 2], res[:, n % 2], xs[:, n * TPB:(n + 1) * TPB, :], ALU.add).then_inc(S["d_nrm"], 1)

        @block.tensor
        def _(pe):
            pe.wait_ge(S["zeroed"], 5)
            pe.wait_ge(S["w_in_ld"], 3 * DMA)
            with pe.Fori(0, BATCH) as bt:
                pe.wait_ge(S["a_xn"], bt + 1)
                for i in range(TPB):
                    last = tr(bank(i // 4, P, (i % 4) * P), xn[:, i, :], ident[:])
                    if i % 4 == 3:
                        last.then_inc(S["a_xt_ps"], 1)
                pe.wait_ge(S["a_xt_a"], bt + 1)
                pe.wait_ge(S["a_xt_v"], bt + 1)
                for j in range(2):
                    mm(bank(2 + j), w_in[:, 0:DIM], xT[:, j * BANK:(j + 1) * BANK], start=True, stop=True).then_inc(S["a_q_ps"], 1)
                for j in range(2):
                    mm(bank(4 + j), w_in[:, DIM:2 * DIM], xT[:, j * BANK:(j + 1) * BANK], start=True, stop=True).then_inc(S["a_k_ps"], 1)
                for i in range(TPB):
                    last = mm(bank(6 + i // 4, DIM, (i % 4) * DIM), xT[:, i * P:(i + 1) * P], w_in[:, 2 * DIM:3 * DIM],
                              start=True, stop=True)
                    if i % 4 == 3:
                        last.then_inc(S["a_v_ps"], 1)
                pe.wait_ge(S["a_qT"], 2 * bt + 2)
                pe.wait_ge(S["a_kT"], 2 * bt + 2)

                def scores(i):
                    if i >= 2:
                        pe.wait_ge(S["a_exp"], bt * TPB + i - 1)
                    n = (i + 1) * P
                    for c in range(0, n, BANK):
                        w = min(BANK, n - c)
                        o = PS[:, (i % 2) * 2 * BANK + c:(i % 2) * 2 * BANK + c + w]
                        last = mm(o, qT[:, i * P:(i + 1) * P], kT[:, c:c + w], start=True, stop=c + w < n)
                    o = PS[:, (i % 2) * 2 * BANK + i * P:(i % 2) * 2 * BANK + n]
                    mm(o, identb[:], causal[:], start=False, stop=True).then_inc(S["a_sc"], 1)

                scores(0)
                pe.wait_ge(S["a_v"], 2 * bt + 2)
                for i in range(TPB):
                    if i + 1 < TPB:
                        scores(i + 1)
                    pe.wait_ge(S["a_exp"], bt * TPB + i + 1)
                    for j in range(i + 1):
                        last = tr(bank(4 + j // 4, P, (j % 4) * P), prob[:, i % 2, j * P:(j + 1) * P], ident[:])
                    last.then_inc(S["a_pt"], 1)
                    pe.wait_ge(S["a_pt_a"], bt * TPB + i + 1)
                    if i >= 4:
                        pe.wait_ge(S["a_pt_v"], bt * 4 + i - 3)
                    if i >= 2:
                        pe.wait_ge(S["a_o"], bt * TPB + i - 1)
                    for j in range(i + 1):
                        last = mm(bank(6 + i % 2, DIM), pT[:, j * P:(j + 1) * P], v_sb[:, j, :], start=(j == 0), stop=(j == i))
                    last.then_inc(S["a_pv"], 1)

            with pe.Fori(0, DEPTH) as l:
                pe.wait_ge(S["stream"], 2 * l + 1)
                pe.wait_ge(S["wl_ld"], DMA * 20 * (l + 1))

                def xt(t, u, first):
                    G = l * TILES + t
                    pe.wait_ge(*h_loaded(l, t, u))
                    if not first:
                        pe.wait_ge(S["v_ok"], G)
                    tr(bank(2, P), h_in[:, u, :], ident[:]).then_inc(S["xt_ps"], 1)

                def qkv(t, first):
                    G = l * TILES + t
                    pe.wait_ge(S["h_t"], G + 1)
                    if not first:
                        pe.wait_ge(S["rot_terms"], G)
                    mm(bank(0), hT, w_qkv[:, 0:INNER], start=True, stop=True).then_inc(S["q_ps"], 1)
                    mm(bank(1), hT, w_qkv[:, INNER:2 * INNER], start=True, stop=True).then_inc(S["k_ps"], 1)
                    mm(bank(2), hT, w_qkv[:, 2 * INNER:], start=True, stop=True).then_inc(S["v_ps"], 1)

                def turn_qk(t):
                    pe.wait_ge(S["qk_ok"], l * TILES + t + 1)
                    for c in range(2 * INNER // P):
                        last = tr(bank(5 + c // 4, P, (c % 4) * P), qk_rot[:, c * P:(c + 1) * P], ident[:])
                    last.then_inc(S["tr_ps"], 1)

                def turn_probs(t):
                    G = l * TILES + t
                    pe.wait_ge(S["probs"], 2 * G + 2)
                    for j in range(HEADS):
                        last = tr(bank(3 + j // 4, P, (j % 4) * P), wprob[:, j, :], ident[:])
                        if j % 4 == 3:
                            last.then_inc(S["pt_ps"], 1)

                def values(t, u, lfirst):
                    G = l * TILES + t
                    pe.wait_ge(S["pt_a"], G + 1)
                    pe.wait_ge(S["pt_v"], G + 1)
                    pe.wait_ge(*hi_shifted(l, t, u))
                    if not lfirst:
                        pe.wait_ge(*lo_shifted(l, t - 1, 1 - u))
                        pe.wait_ge(S["updated"], G)
                    for j in range(HEADS):
                        h = head(j)
                        c = slice(h * DH, (h + 1) * DH)
                        mm(bank(7, DH, h * DH)[0:WINDOW], wpT[:, j, 0:WINDOW], wvs[:, u, c], start=True, stop=True)
                        last = mm(bank(7, DH, h * DH)[WINDOW:P], wpT[:, j, WINDOW:P], wv[:, u, c], start=True, stop=True)
                    last.then_inc(S["o_ps"], 1)

                def wscores(t, u):
                    G = l * TILES + t
                    pe.wait_ge(S["qk_t"], G + 1)
                    if isinstance(t, int):
                        sel = 0 if t % TPB == 0 else 1
                        msk = band[:, sel, :]
                    else:
                        sel = bounded(((t & (TPB - 1)) + (TPB - 1)) >> 3, 0, 1)
                        msk = band[:, bass.ds(sel, 1), :].rearrange("p a c -> p (a c)")
                    for half in range(2):
                        mm(bank(3 + half), identb[:], msk, start=True, stop=False)
                        for j in range(half * 4, half * 4 + 4):
                            h = head(j)
                            r, g = slice((h % 2) * DH, (h % 2 + 1) * DH), h // 2
                            o = bank(3 + half, P, (j % 4) * P)
                            mm(o[0:WINDOW], wqT[r, g, 0:WINDOW], wkT[r, u, g, 0:P], start=False, stop=(j % 4 == 3))
                            last = mm(o[WINDOW:P], wqT[r, g, WINDOW:P], wkT[r, u, g, WINDOW:], start=False, stop=(j % 4 == 3))
                        last.then_inc(S["sc_ps"], 1)

                def turn_o(t):
                    pe.wait_ge(S["o_ok"], l * TILES + t + 1)
                    for c in range(INNER // P):
                        last = tr(bank(5, P, c * P), o_n[:, c * P:(c + 1) * P], ident[:])
                    last.then_inc(S["ot_ps"], 1)

                def project(t):
                    pe.wait_ge(S["ot_ok"], l * TILES + t + 1)
                    for c in range(INNER // P):
                        last = mm(bank(7, DIM), oT[:, c, :], w_o[:, c, :], start=(c == 0), stop=(c == INNER // P - 1))
                    last.then_inc(S["wo_ps"], 1)

                def slot(t, u, first=False, second=False, last=False, end=False):
                    if not (last or end):
                        xt(t + 1, 1 - u, False)
                    if not end:
                        turn_qk(t)
                    if not (last or end):
                        qkv(t + 1, False)
                    if not first:
                        turn_probs(t - 1)
                        values(t - 1, 1 - u, second)
                    if not end:
                        wscores(t, u)
                    if not first:
                        turn_o(t - 1)
                        project(t - 1)

                xt(0, 0, True)
                qkv(0, True)
                slot(0, 0, first=True)
                slot(1, 1, second=True)
                slot(2, 0)
                with pe.Fori(1, TILES // 2 - 1) as p:
                    slot(2 * p + 1, 1)
                    slot(2 * p + 2, 0)
                slot(TILES - 1, 1, last=True)
                slot(TILES, 0, end=True)

                pe.wait_ge(S["stream"], 2 * l + 2)

                def turn_h(g, gu, first=False):
                    G = l * GROUPS + g
                    pe.wait_ge(S["c_hn"], G + 1)
                    if not first:
                        pe.wait_ge(S["c_hid"], NB * (G - 1) + 1)
                    for i in range(GT):
                        last = tr(bank(2, P, i * P), hc[:, gu, i, :], ident[:])
                    last.then_inc(S["c_t_ps"], 1)

                def up(g, gu, first=False):
                    G = l * GROUPS + g
                    pe.wait_ge(S["c_hT"], G + 1)
                    for m, (o, n) in enumerate(HBLK):
                        if not first:
                            pe.wait_ge(S["c_hid"], NB * (G - 1) + m + 1)
                        mm(bank(2 + m)[0:n], w_1[:, o:o + n], hcT, start=True, stop=True)
                        mm(bank(5 + m)[0:n], w_1[:, HID + o:HID + o + n], hcT, start=True, stop=True).then_inc(S["c_g_ps"], 1)

                def down(g, gu, half):
                    G = l * GROUPS + g
                    if half == 0:
                        pe.wait_ge(S["c_hid"], NB * (G + 1))
                        pe.wait_ge(S["c_out_free"], G + 1)
                    for i in range(2 * half, 2 * half + 2):
                        for m, (o, n) in enumerate(HBLK):
                            n += m == NB - 1
                            last = mm(bank(gu, DIM, i * DIM), hid[0:n, gu * NB + m, i * P:(i + 1) * P], w_2[0:n, m, :],
                                      start=(m == 0), stop=(m == NB - 1))
                    if half:
                        last.then_inc(S["c_out_ps"], 1)

                def gslot(g, gu, first=False, last=False):
                    up(g, gu, first)
                    if not first:
                        down(g - 1, 1 - gu, 0)
                    if not last:
                        turn_h(g + 1, 1 - gu)
                    if not first:
                        down(g - 1, 1 - gu, 1)

                turn_h(0, 0, first=True)
                gslot(0, 0, first=True)
                with pe.Fori(0, GROUPS // 2 - 1) as p:
                    gslot(2 * p + 1, 1)
                    gslot(2 * p + 2, 0)
                gslot(GROUPS - 1, 1, last=True)
                down(GROUPS - 1, 1, 0)
                down(GROUPS - 1, 1, 1)


_INS = ['L0_attn_x', 'L0_attn_W', 'L0_attn_b', 'L0_ffn_wqkv', 'L0_ffn_q_scale', 'L0_ffn_k_scale', 'L0_ffn_wo',
        'L0_ffn_ln_g', 'L0_ffn_ln_b', 'L0_ffn_w1', 'L0_ffn_b1', 'L0_ffn_w2', 'L0_ffn_b2']


def xpos_tables():
    import numpy as np
    f = np.float32
    half_idx = np.arange(0, DH, 2, dtype=f)
    inv_freq = (f(1.0) / np.power(f(10000.0), half_idx / f(DH))).astype(f)
    t = np.arange(SEQ, dtype=f)
    freqs = t[:, None] * inv_freq[None, :]
    base = (half_idx + f(0.4 * DH)) / f(1.4 * DH)
    power = (t - f(SEQ // 2)) / f(WINDOW // 2)
    scale = np.power(base[None, :], power[:, None]).astype(f)
    cos, sin = np.cos(freqs).astype(f), np.sin(freqs).astype(f)
    q8 = f(QK_SCALE)
    rows = [np.concatenate([cos * scale * q8] * 2, -1), np.concatenate([cos / scale] * 2, -1),
            np.concatenate([-sin * scale * q8, sin * scale * q8], -1), np.concatenate([-sin / scale, sin / scale], -1)]
    tab = np.stack(rows, 1).astype(f)
    return np.ascontiguousarray(tab.reshape(TPB, P, 4, DH).transpose(1, 0, 2, 3))


def kernel(**inputs):
    import numpy as _np
    import concourse.bacc as _bacc
    from concourse.bass_utils import run_bass_kernel_spmd as _run

    nc = _bacc.Bacc("TRN2", target_bir_lowering=False, num_devices=1)
    arrays, args = {}, []
    for name in _INS:
        a = _np.ascontiguousarray(inputs[name])
        arrays[f"in_{name}"] = a
        args.append(nc.dram_tensor(f"in_{name}", a.shape, mybir.dt.from_np(a.dtype), kind="ExternalInput").ap())
    tables = xpos_tables()
    arrays["xpos"] = tables
    args.append(nc.dram_tensor("xpos", tables.shape, mybir.dt.from_np(tables.dtype), kind="ExternalInput").ap())
    out = nc.dram_tensor("out_0", (BATCH, SEQ, DIM), mybir.dt.float32, kind="ExternalOutput").ap()
    build_program(nc, *args, out)
    r = _run(nc, [arrays], core_ids=[0])
    return r.results[0]["out_0"]
```

```python
import concourse.bass as bass
from concourse import mybir
from contextlib import ExitStack

P = 128
BATCH = 8
SEQ = 1024
DIM = 128
TPB = SEQ // P
TILES = BATCH * TPB
DEPTH = 2
HEADS = 8
DH = 64
INNER = HEADS * DH
WINDOW = 64
HALF = DH // 2
HID = int(DIM * 4 * 2 / 3)
HBLK = [(0, P), (P, P), (2 * P, HID - 2 * P)]
NB = len(HBLK)
TAIL = HBLK[-1][1]
GT = 4
GROUPS = TILES // GT
BANK = 512
LN_EPS = 1e-5
NORM_MIN2 = 1e-24
ATT_SCALE = float(DIM) ** -0.5
QK_SCALE = 8.0
NEG = -3.0e38
DMA = 16


def build_program(nc, x, W, b, wqkv, q_scale, k_scale, wo, ln_g, ln_b, w1, b1, w2, b2, xpos, out):
    f32, bf16 = mybir.dt.float32, mybir.dt.bfloat16
    ALU, ACT, AX = mybir.AluOpType, mybir.ActivationFunctionType, mybir.AxisListType
    mm, tr = nc.tensor.matmul, nc.tensor.transpose

    with ExitStack() as ctx:
        def sb(name, shape, dt=f32):
            return ctx.enter_context(nc.sbuf_tensor(name, shape, dt))

        def sem(name):
            return ctx.enter_context(nc.semaphore(name))

        xs = sb("xs", [P, TILES, DIM])
        ys = sb("ys", [P, BATCH * (TPB + 1), DIM])
        ident = sb("ident", [P, P])
        identb = sb("identb", [P, P], bf16)
        causal = sb("causal", [P, P], bf16)
        band = sb("band", [P, 2, BANK], bf16)
        carrier = sb("carrier", [P, 1])
        eps = sb("eps", [P, TPB])
        half_neg = sb("half_neg", [P, 2 * HEADS])
        w_in = sb("w_in", [P, 3 * DIM])
        b_col = sb("b_col", [P, 2])
        bv_all = sb("bv_all", [P, DIM])
        region = sb("region", [P, 16896])
        used = [0]

        def part(*shape):
            n = 1
            for s in shape:
                n *= s
            v = region[:, used[0]:used[0] + n]
            used[0] += n
            assert used[0] <= 16896, used[0]
            if len(shape) == 2:
                v = v.rearrange("p (a b) -> p a b", a=shape[0])
            if len(shape) == 3:
                v = v.rearrange("p (a b c) -> p a b c", a=shape[0], b=shape[1])
            return v

        st = sb("st", [P, TPB, 6])
        mv = sb("mv", [P, TPB, 2])
        rstd = sb("rstd", [P, TPB])

        xn = part(TPB, DIM)
        xT = part(SEQ)
        qT = part(SEQ)
        kT = part(SEQ)
        v_sb = part(TPB, DIM)
        prob = part(2, SEQ)
        pT = part(SEQ)
        o_sb = part(TPB, DIM)
        negmax = sb("negmax", [P, 2])
        rowsum = sb("rowsum", [P, 2])
        rinv = sb("rinv", [P, 2])

        used[0] = 0
        w_qkv = sb("w_qkv", [P, 3 * INNER])
        w_o = sb("w_o", [P, INNER // P, DIM])
        base = sb("base", [P, TPB, 4, DH])
        tab = sb("tab", [P, TPB, 4, DH])
        qks = sb("qks", [P, 4, DH])
        h_in = part(2, DIM)
        hT = part(P)
        sq = part(2 * INNER)
        termA = part(2 * INNER)
        termB = part(2 * INNER)
        rsum = part(2 * INNER)
        qk_rot = part(2 * INNER)
        wqT = part(HEADS // 2, P)
        wkT = part(2, HEADS // 2, P + WINDOW)
        wv = part(2, INNER)
        wvs = part(2, INNER)
        wprob = part(HEADS, P)
        wpT = part(HEADS, P)
        o_n = part(INNER)
        oT = part(HEADS // 2, P)
        ss = sb("ss", [P, 2 * HEADS])
        rr = sb("rr", [P, 2 * HEADS])
        wnegmax = sb("wnegmax", [P, HEADS])
        wrowsum = sb("wrowsum", [P, 2, HEADS])
        wrinv = sb("wrinv", [P, HEADS])

        used[0] = 0
        w_1 = sb("w_1", [P, 2 * HID])
        w_2 = sb("w_2", [P, NB, DIM])
        b_1 = sb("b_1", [P, 2, NB])
        ln_cols = sb("ln_cols", [P, 2])
        hc = part(2, GT, DIM)
        hcT = part(GT * P)
        gel = part(NB, GT * P)
        hid = part(2 * NB, GT * P)
        fst = sb("fst", [P, GT, 6])
        fmv = sb("fmv", [P, GT, 2])
        frs = sb("frs", [P, GT])
        used[0] = 0
        res = part(2, TPB, DIM)

        PS = ctx.enter_context(nc.psum_tensor("PS", [P, 8 * BANK], f32))

        def bank(n, cols=BANK, off=0):
            return PS[:, n * BANK + off:n * BANK + off + cols]

        names = """consts iota0 w_in_ld wl_ld x_ld zeroed
            n_step n_mv n_rstd o_step o_mv o_rstd on_step x1_step y_step y_mv y_rstd a_xn a_xt_ps a_xt a_q_ps a_k_ps a_v_ps a_qT a_kT a_v
            a_sc a_nm a_exp a_pt a_pt_a a_pt_v a_pv a_o a_bcol
            dve_step pool_step stream
            h_ld0 h_ld1 xt_ps h_t q_ps k_ps v_ps sq_ok ss_sum ss_ok rr_ok rot_terms rot_sum qk_ok tr_ps qk_t sc_ps nm_ok
            probs pt_ps pt_a pt_v v_ok vs_hi0 vs_hi1 vs_lo0 vs_lo1 o_ps o_ok ot_ps ot_ok wo_ps
            hc_ld0 hc_ld1 c_mv c_rs c_hn c_t_ps c_hT c_g_ps c_gel c_hid c_out_ps c_out_free
            d_mv d_rs d_nrm d_st0 d_st1 a_y a_rinv updated""".split()
        S = {n: sem(n) for n in names}

        def head(j):
            return 2 * (j % (HEADS // 2)) + j // (HEADS // 2)

        def h_loaded(l, t, u):
            return S[f"h_ld{u}"], 3 * DMA * (l * (TILES // 2) + (t >> 1) + 1)

        def hi_shifted(l, t, u):
            return S[f"vs_hi{u}"], DMA * (l * (TILES // 2) + (t >> 1) + 1)

        def lo_shifted(l, t, u):
            return S[f"vs_lo{u}"], DMA * (l * (TILES // 2 - u) + (t >> 1) + 1)

        def group_loaded(l, g, u):
            return S[f"hc_ld{u}"], 3 * DMA * (l * (GROUPS // 2) + (g >> 1) + 1)

        def bounded(v, low, high):
            return v.with_bounds(min_val=low, max_val=high)

        def yslot(t):
            if isinstance(t, int):
                return t + t // TPB + 1
            return bounded(t + (t >> 3) + 1, 1, BATCH * (TPB + 1) - 1)

        block = ctx.enter_context(nc.Block())
        x_t = x.rearrange("b (i p) c -> b p i c", p=P)
        out_t = out.rearrange("b (i p) c -> b p i c", p=P)

        @block.sync
        def _(sp):
            sp.dma_start(w_in[:], W).then_inc(S["w_in_ld"], DMA)
            sp.dma_start(b_col[:], b[0:2 * DIM].rearrange("(s c) -> c s", s=2),
                         allow_slow_non_contiguous=True).then_inc(S["w_in_ld"], DMA)
            sp.dma_start(bv_all[:], b[2 * DIM:3 * DIM].partition_broadcast(P)).then_inc(S["w_in_ld"], DMA)
            for n in range(BATCH):
                if n:
                    sp.wait_ge(S["x_ld"], DMA * n)
                sp.dma_start(xs[:, n * TPB:(n + 1) * TPB, :], x_t[n]).then_inc(S["x_ld"], DMA)
            sp.dma_start(base[:], xpos).then_inc(S["consts"], DMA)

            def shifted(l, t, u, free=None):
                s = sp.snap(yslot(t)) if free is not None else yslot(t)
                if free is not None:
                    sp.wait_ge(S["xt_ps"], free)
                sp.dma_start(h_in[:, u, 0:DIM // 2], ys[:, bass.ds(s, 1), 0:DIM // 2]).then_inc(S[f"h_ld{u}"], DMA)
                sp.dma_start(h_in[1:P, u, DIM // 2:], ys[0:P - 1, bass.ds(s, 1), DIM // 2:]).then_inc(S[f"h_ld{u}"], DMA)
                sp.dma_start(h_in[0:1, u, DIM // 2:], ys[P - 1:P, bass.ds(s - 1, 1), DIM // 2:]).then_inc(S[f"h_ld{u}"], DMA)

            def v_shift(l, t, u, first, last):
                G = l * TILES + t
                sp.wait_ge(S["v_ok"], G + 1)
                sp.dma_start(wvs[WINDOW:P, u, :], wv[0:WINDOW, u, :]).then_inc(S[f"vs_hi{u}"], DMA)
                if not last:
                    if not first:
                        sp.wait_ge(S["o_ps"], G)
                    sp.dma_start(wvs[0:WINDOW, 1 - u, :], wv[WINDOW:P, u, :]).then_inc(S[f"vs_lo{u}"], DMA)

            def shifted_group(l, bt, gu):
                s = bt * (TPB + 1) + 1 + gu * GT
                sp.dma_start(hc[:, gu, :, 0:DIM // 2], ys[:, bass.ds(s, GT), 0:DIM // 2]).then_inc(S[f"hc_ld{gu}"], DMA)
                sp.dma_start(hc[1:P, gu, :, DIM // 2:], ys[0:P - 1, bass.ds(s, GT), DIM // 2:]).then_inc(S[f"hc_ld{gu}"], DMA)
                sp.dma_start(hc[0:1, gu, :, DIM // 2:], ys[P - 1:P, bass.ds(s - 1, GT), DIM // 2:]).then_inc(S[f"hc_ld{gu}"], DMA)

            with sp.Fori(0, DEPTH) as l:
                sp.wait_ge(S["stream"], 2 * l + 1)
                loads = [
                    (w_qkv[:], wqkv[bass.ds(l, 1)].rearrange("a c n -> (a c) n")),
                    (w_o[:], wo[bass.ds(l, 1)].rearrange("a (k c) n -> (a c) k n", c=P)),
                    (w_1[:], w1[bass.ds(l, 1)].rearrange("a c n -> (a c) n")),
                    (w_2[:, 0:2, :], w2[bass.ds(l, 1), 0:2 * P].rearrange("a (k c) n -> (a c) k n", c=P)),
                    (w_2[0:TAIL, 2, :], w2[bass.ds(l, 1), 2 * P:HID].rearrange("a c n -> (a c) n")),
                    (w_2[TAIL:TAIL + 1, 2, :], b2[bass.ds(l, 1)]),
                    (ln_cols[:, 0:1], ln_g[bass.ds(l, 1)].rearrange("a c -> c a")),
                    (ln_cols[:, 1:2], ln_b[bass.ds(l, 1)].rearrange("a c -> c a")),
                    (qks[:, 0, :], q_scale[bass.ds(l, 1)].rearrange("a c -> (a c)").partition_broadcast(P)),
                    (qks[:, 1, :], k_scale[bass.ds(l, 1)].rearrange("a c -> (a c)").partition_broadcast(P)),
                ]
                for s, scale in ((2, q_scale), (3, k_scale)):
                    for h in range(2):
                        loads.append((qks[:, s, h * HALF:(h + 1) * HALF],
                                      scale[bass.ds(l, 1), (1 - h) * HALF:(2 - h) * HALF]
                                      .rearrange("a c -> (a c)").partition_broadcast(P)))
                for s in range(2):
                    for m, (o, n) in enumerate(HBLK):
                        loads.append((b_1[0:n, s, m:m + 1],
                                      b1[bass.ds(l, 1), s * HID + o:s * HID + o + n].rearrange("a c -> c a")))
                for dst, src in loads:
                    sp.dma_start(dst, src, allow_slow_non_contiguous=True).then_inc(S["wl_ld"], DMA)

                shifted(l, 0, 0)
                shifted(l, 1, 1)
                def ahead(t, u):
                    shifted(l, t + 2, u, l * TILES + t + 1)

                ahead(0, 0)
                v_shift(l, 0, 0, True, False)
                with sp.Fori(0, TILES // 2 - 2) as p:
                    for k in (1, 2):
                        ahead(2 * p + k, k % 2)
                        v_shift(l, 2 * p + k, k % 2, False, False)
                ahead(TILES - 3, 1)
                v_shift(l, TILES - 3, 1, False, False)
                v_shift(l, TILES - 2, 0, False, False)
                v_shift(l, TILES - 1, 1, False, True)

                sp.wait_ge(S["stream"], 2 * l + 2)
                shifted_group(l, 0, 0)
                shifted_group(l, 0, 1)
                with sp.Fori(1, BATCH) as bt:
                    for gu in range(2):
                        sp.wait_ge(S["c_t_ps"], l * GROUPS + 2 * bt + gu - 1)
                        shifted_group(l, bt, gu)

            for n in range(BATCH):
                sp.wait_ge(S["d_nrm"], n + 1)
                sp.dma_start(out_t[n], res[:, n % 2]).then_inc(S[f"d_st{n % 2}"], DMA)
            for u in range(2):
                sp.wait_ge(S[f"d_st{u}"], DMA * BATCH // 2)

        @block.gpsimd
        def _(pool):
            pool.memset(ident[:], 0.0).then_inc(S["iota0"], 1)
            pool.memset(causal[:], 0.0).then_inc(S["iota0"], 1)
            pool.memset(band[:], 0.0).then_inc(S["iota0"], 1)
            pool.memset(half_neg[:], -0.5)
            pool.memset(eps[:], LN_EPS).then_inc(S["zeroed"], 1)
            pool.memset(ys[:, :, :].rearrange("p (n i) c -> p n i c", n=BATCH)[:, :, 0, :], 0.0).then_inc(S["zeroed"], 1)
            pool.wait_ge(S["iota0"], 3)
            pool.affine_select(out=ident[:], in_=ident[:], compare_op=ALU.not_equal, fill=1.0, base=0,
                               pattern=[[-1, P]], channel_multiplier=1).then_inc(S["iota0"], 1)
            pool.affine_select(out=causal[:], in_=causal[:], compare_op=ALU.is_ge, fill=NEG, base=0,
                               pattern=[[-1, P]], channel_multiplier=1).then_inc(S["zeroed"], 1)
            n = 4
            for lo in (0, WINDOW):
                rows = band[lo:lo + WINDOW].rearrange("p s (h c) -> p (s h) c", c=P)
                pool.wait_ge(S["iota0"], n)
                pool.affine_select(out=rows, in_=rows, compare_op=ALU.is_ge, fill=NEG, base=0,
                                   pattern=[[0, 2 * BANK // P], [1, P]], channel_multiplier=-1).then_inc(S["iota0"], 1)
                n += 1
                pool.wait_ge(S["iota0"], n)
                pool.affine_select(out=rows, in_=rows, compare_op=ALU.is_ge, fill=NEG, base=WINDOW,
                                   pattern=[[0, 2 * BANK // P], [-1, P]], channel_multiplier=1).then_inc(S["iota0"], 1)
                n += 1
            pool.wait_ge(S["iota0"], n)
            pool.memset(band[0:WINDOW, 0, :].rearrange("p (h c) -> p h c", c=P)[:, :, 0:WINDOW], NEG).then_inc(S["zeroed"], 1)

            def rsqrt(dst, src, wait, done, n):
                pool.wait_ge(S[wait[0]], wait[1])
                pool.tensor_tensor(dst, src, eps[:, 0:n], ALU.add).then_inc(S["pool_step"], 1)
                pool.wait_ge(S["pool_step"], pstep(1))
                pool.tensor_tensor(dst, dst, half_neg[:, 0:n], ALU.pow).then_inc(S[done], 1)

            def pstep(k):
                return pcount[0] + k
            pcount = [0]
            pool.wait_ge(S["zeroed"], 5)

            def tile_rsqrt(k, name, n, step):
                pcount[0] = step
                rsqrt(rstd[:, k:k + 1], mv[:, k, 1:2], (f"{name}_mv", n + 1), f"{name}_rstd", 1)

            for i in range(TPB):
                tile_rsqrt(0, "n", i, i)

            def first_attention(bt, more):
                N, steps = bt * TPB, TPB + 3 * TPB * bt
                for i in range(TPB + 1):
                    order = []
                    if i:
                        order.append((1, "o", N + i - 1))
                    if more and i < TPB:
                        order.append((0, "n", N + TPB + i))
                    if i:
                        order.append((2, "y", N + i - 1))
                    for k, name, n in order:
                        tile_rsqrt(k, name, n, steps)
                        steps = steps + 1

            with pool.Fori(0, BATCH - 1) as bt:
                first_attention(bt, True)
            first_attention(BATCH - 1, False)

            with pool.Fori(0, DEPTH) as l:
                def norms(t, first):
                    G = l * TILES + t
                    pool.wait_ge(S["ss_ok"], G + 1)
                    if not first:
                        pool.wait_ge(S["qk_ok"], G)
                    pool.tensor_tensor(rr[:], ss[:], half_neg[:], ALU.pow).then_inc(S["rr_ok"], 1)
                    pool.wait_ge(S["rot_terms"], G + 1)
                    pool.tensor_tensor(rsum[:], termA[:], termB[:], ALU.add).then_inc(S["rot_sum"], 1)

                norms(0, True)
                with pool.Fori(0, TILES // 2 - 1) as p:
                    norms(2 * p + 1, False)
                    norms(2 * p + 2, False)
                norms(TILES - 1, False)
                with pool.Fori(0, GROUPS) as g:
                    pcount[0] = 3 * TILES + l * GROUPS + g
                    rsqrt(frs[:], fmv[:, :, 1], ("c_mv", l * GROUPS + g + 1), "c_rs", GT)

            for n in range(BATCH):
                pcount[0] = 3 * TILES + DEPTH * GROUPS + n
                rsqrt(rstd[:], mv[:, :, 1], ("d_mv", n + 1), "d_rs", TPB)

        @block.scalar
        def _(act):
            A = act.activation
            act.wait_ge(S["a_bcol"], 1)
            def first_attention(bt):
                for j in range(2):
                    act.wait_ge(S["a_xt_ps"], 2 * bt + j + 1)
                    A(xT[:, j * BANK:(j + 1) * BANK], bank(j), ACT.Copy).then_inc(S["a_xt"], 1)
                for j in range(2):
                    act.wait_ge(S["a_q_ps"], 2 * bt + j + 1)
                    A(qT[:, j * BANK:(j + 1) * BANK], bank(2 + j), ACT.Identity, bias=b_col[:, 0:1],
                      scale=ATT_SCALE).then_inc(S["a_qT"], 1)
                for j in range(2):
                    act.wait_ge(S["a_k_ps"], 2 * bt + j + 1)
                    A(kT[:, j * BANK:(j + 1) * BANK], bank(4 + j), ACT.Identity, bias=b_col[:, 1:2]).then_inc(S["a_kT"], 1)

                def exps(i):
                    n = (i + 1) * P
                    act.wait_ge(S["a_nm"], bt * TPB + i + 1)
                    A(prob[:, i % 2, 0:n], PS[:, (i % 2) * 2 * BANK:(i % 2) * 2 * BANK + n], ACT.Exp,
                      bias=negmax[:, i % 2:i % 2 + 1], accum_out=rowsum[:, i % 2:i % 2 + 1]).then_inc(S["a_exp"], 1)

                exps(0)
                for i in range(TPB):
                    if i + 1 < TPB:
                        exps(i + 1)
                    act.wait_ge(S["a_pt"], bt * TPB + i + 1)
                    n = min((i + 1) * P, BANK)
                    A(pT[:, 0:n], bank(4, n), ACT.Copy).then_inc(S["a_pt_a"], 1)
                    act.wait_ge(S["a_rinv"], bt * TPB + i + 1)
                    act.wait_ge(S["a_pv"], bt * TPB + i + 1)
                    A(o_sb[:, i, :], bank(6 + i % 2, DIM), ACT.Copy, scale=rinv[:, i % 2:i % 2 + 1]).then_inc(S["a_o"], 1)

            with act.Fori(0, BATCH) as bt:
                first_attention(bt)

            with act.Fori(0, DEPTH) as l:
                act.wait_ge(S["stream"], 2 * l + 1)

                def h_evac(t):
                    act.wait_ge(S["xt_ps"], l * TILES + t + 1)
                    A(hT, bank(2, P), ACT.Copy).then_inc(S["h_t"], 1)

                def squares(t, first):
                    G = l * TILES + t
                    if not first:
                        act.wait_ge(S["ss_ok"], G)
                    for s, ps in enumerate(("q_ps", "k_ps")):
                        act.wait_ge(S[ps], G + 1)
                        A(sq[:, s * INNER:(s + 1) * INNER], bank(s), ACT.Square).then_inc(S["sq_ok"], 1)

                def v_evac(t, u, early):
                    G = l * TILES + t
                    act.wait_ge(S["v_ps"], G + 1)
                    if not early:
                        act.wait_ge(S["o_ps"], G - 1)
                        act.wait_ge(*hi_shifted(l, t - 2, u))
                        act.wait_ge(*lo_shifted(l, t - 2, u))
                    A(wv[:, u, :], bank(2), ACT.Copy).then_inc(S["v_ok"], 1)

                def exps(t, u, half):
                    G = l * TILES + t
                    act.wait_ge(S["nm_ok"], 2 * G + half + 1)
                    for j in range(half * 4, half * 4 + 4):
                        last = A(wprob[:, j, :], bank(3 + half, P, (j % 4) * P), ACT.Exp,
                                 bias=wnegmax[:, j:j + 1], accum_out=wrowsum[:, u, head(j):head(j) + 1])
                    last.then_inc(S["probs"], 1)

                def qk_evac(t, u):
                    act.wait_ge(S["tr_ps"], l * TILES + t + 1)
                    A(wqT, bank(5), ACT.Copy)
                    kps = bank(6).rearrange("p (g c) -> p g c", c=P)
                    A(wkT[:, u, :, WINDOW:], kps, ACT.Copy)
                    A(wkT[:, 1 - u, :, 0:WINDOW], kps[:, :, P - WINDOW:], ACT.Copy).then_inc(S["qk_t"], 1)

                def pt_evac(t):
                    act.wait_ge(S["pt_ps"], 2 * (l * TILES + t) + 1)
                    A(wpT[:, 0:4, :], bank(3), ACT.Copy).then_inc(S["pt_a"], 1)

                def ot_evac(t):
                    act.wait_ge(S["ot_ps"], l * TILES + t + 1)
                    A(oT, bank(5), ACT.Copy).then_inc(S["ot_ok"], 1)

                def slot(t, u, before=True, after=2):
                    if after >= 2:
                        h_evac(t + 2)
                    exps(t, u, 0)
                    exps(t, u, 1)
                    if before:
                        ot_evac(t - 1)
                    if after >= 2:
                        squares(t + 2, False)
                    pt_evac(t)
                    if after >= 1:
                        qk_evac(t + 1, 1 - u)
                    if after >= 2:
                        v_evac(t + 2, u, False)

                h_evac(0)
                squares(0, True)
                v_evac(0, 0, True)
                h_evac(1)
                qk_evac(0, 0)
                squares(1, False)
                v_evac(1, 1, True)
                slot(0, 0, before=False)
                with act.Fori(0, TILES // 2 - 2) as p:
                    slot(2 * p + 1, 1)
                    slot(2 * p + 2, 0)
                slot(TILES - 3, 1)
                slot(TILES - 2, 0, after=1)
                slot(TILES - 1, 1, after=0)
                ot_evac(TILES - 1)

                act.wait_ge(S["stream"], 2 * l + 2)

                def hT_evac(g):
                    act.wait_ge(S["c_t_ps"], l * GROUPS + g + 1)
                    A(hcT, bank(2), ACT.Identity, bias=ln_cols[:, 1:2], scale=ln_cols[:, 0:1]).then_inc(S["c_hT"], 1)

                def gelus(g):
                    for m, (o, n) in enumerate(HBLK):
                        act.wait_ge(S["c_g_ps"], NB * (l * GROUPS + g) + m + 1)
                        A(gel[0:n, m, :], bank(5 + m)[0:n], ACT.Gelu, bias=b_1[0:n, 1, m:m + 1]).then_inc(S["c_gel"], 1)

                hT_evac(0)
                with act.Fori(0, GROUPS - 1) as g:
                    gelus(g)
                    hT_evac(g + 1)
                gelus(GROUPS - 1)

        @block.vector
        def _(dve):
            V = nc.vector

            def wait_then_go(semaphore, value):
                dve.wait_ge(semaphore, value)
                V.memset(carrier[:], 0.0)

            def stats(dst_mv, dst_st, tiles, n, base_count, s="dve_step"):
                for i in range(n):
                    last = V.bn_stats(dst_st[:, i, :], tiles(i))
                last.then_inc(S[s], 1)
                wait_then_go(S[s], base_count + 1)
                for i in range(n):
                    last = V.bn_aggr(dst_mv[:, i, :], dst_st[:, i, :])
                return last

            dve.sem_inc(S["c_out_free"], 2)
            dve.wait_ge(S["w_in_ld"], 3 * DMA)
            V.tensor_scalar(b_col[:, 0:1], b_col[:, 0:1], ATT_SCALE, None, ALU.mult).then_inc(S["a_bcol"], 1)
            dve.wait_ge(S["iota0"], 4)
            V.tensor_copy(identb[:], ident[:]).then_inc(S["zeroed"], 1)
            dve.wait_ge(S["zeroed"], 5)
            xt_ = lambda bt, i: xs[:, bass.ds(bt * TPB + i, 1), :].rearrange("p a c -> p (a c)")
            yt_ = lambda bt, i: ys[:, bass.ds(bt * (TPB + 1) + 1 + i, 1), :].rearrange("p a c -> p (a c)")
            def first_norm(bt, i, n):
                V.bn_stats(st[:, 0, :], xt_(bt, i)).then_inc(S["n_step"], 1)
                wait_then_go(S["n_step"], n + 1)
                V.bn_aggr(mv[:, 0, :], st[:, 0, :]).then_inc(S["n_mv"], 1)

            def first_apply(bt, i, n):
                dve.wait_ge(S["n_rstd"], n + 1)
                return V.tensor_scalar(xn[:, i, :], xt_(bt, i), mv[:, 0, 0:1], rstd[:, 0:1], ALU.subtract, ALU.mult)

            dve.wait_ge(S["x_ld"], DMA)
            for i in range(TPB):
                first_norm(0, i, i)
                last = first_apply(0, i, i)
            last.then_inc(S["a_xn"], 1)

            def first_attention(bt, more):
                N = bt * TPB
                if more:
                    dve.wait_ge(S["x_ld"], DMA * (bt + 2))
                for j in range(2):
                    dve.wait_ge(S["a_v_ps"], 2 * bt + j + 1)
                    V.tensor_tensor(v_sb[:, 4 * j:4 * j + 4, :], bank(6 + j).rearrange("p (i c) -> p i c", c=DIM),
                                    bv_all[:].unsqueeze(1).broadcast_to([P, 4, DIM]), ALU.add).then_inc(S["a_v"], 1)

                def rowmax(i):
                    dve.wait_ge(S["a_sc"], N + i + 1)
                    V.tensor_reduce(negmax[:, i % 2:i % 2 + 1],
                                    PS[:, (i % 2) * 2 * BANK:(i % 2) * 2 * BANK + (i + 1) * P], AX.X, ALU.max,
                                    negate=True).then_inc(S["a_nm"], 1)

                def o_stats(i):
                    dve.wait_ge(S["a_o"], N + i + 1)
                    V.bn_stats(st[:, 1, :], o_sb[:, i, :]).then_inc(S["o_step"], 1)

                def o_aggr(i):
                    V.bn_aggr(mv[:, 1, :], st[:, 1, :]).then_inc(S["o_mv"], 1)

                def o_apply(i):
                    dve.wait_ge(S["o_rstd"], N + i + 1)
                    V.tensor_scalar(o_sb[:, i, :], o_sb[:, i, :], mv[:, 1, 0:1], rstd[:, 1:2],
                                    ALU.subtract, ALU.mult).then_inc(S["on_step"], 1)

                def x1_sum(i):
                    dve.wait_ge(S["on_step"], N + i + 1)
                    V.tensor_tensor(xt_(bt, i), xt_(bt, i), o_sb[:, i, :], ALU.add).then_inc(S["x1_step"], 1)

                def y_stats(i):
                    wait_then_go(S["x1_step"], N + i + 1)
                    V.bn_stats(st[:, 2, :], xt_(bt, i)).then_inc(S["y_step"], 1)

                def y_aggr(i):
                    wait_then_go(S["y_step"], N + i + 1)
                    V.bn_aggr(mv[:, 2, :], st[:, 2, :]).then_inc(S["y_mv"], 1)

                def y_apply(i):
                    dve.wait_ge(S["y_rstd"], N + i + 1)
                    V.tensor_scalar(yt_(bt, i), xt_(bt, i), mv[:, 2, 0:1], rstd[:, 2:3],
                                    ALU.subtract, ALU.mult).then_inc(S["a_y"], 1)

                rowmax(0)
                for i in range(TPB):
                    if i:
                        o_stats(i - 1)
                    if i + 1 < TPB:
                        rowmax(i + 1)
                    dve.wait_ge(S["a_exp"], N + i + 1)
                    V.reciprocal(rinv[:, i % 2:i % 2 + 1], rowsum[:, i % 2:i % 2 + 1]).then_inc(S["a_rinv"], 1)
                    if i:
                        wait_then_go(S["o_step"], N + i)
                        o_aggr(i - 1)
                    if i >= 4:
                        dve.wait_ge(S["a_pt"], N + i + 1)
                        V.tensor_copy(pT[:, BANK:(i + 1) * P], bank(5, (i + 1) * P - BANK)).then_inc(S["a_pt_v"], 1)
                    if more:
                        first_norm(bt + 1, i, N + TPB + i)
                    if i:
                        o_apply(i - 1)
                        x1_sum(i - 1)
                        y_stats(i - 1)
                        y_aggr(i - 1)
                    if more:
                        last = first_apply(bt + 1, i, N + TPB + i)
                        if i == TPB - 1:
                            last.then_inc(S["a_xn"], 1)
                    if i:
                        y_apply(i - 1)
                i = TPB - 1
                o_stats(i)
                wait_then_go(S["o_step"], N + i + 1)
                for part_ in (o_aggr, o_apply, x1_sum, y_stats, y_aggr, y_apply):
                    part_(i)

            with dve.Fori(0, BATCH - 1) as bt:
                first_attention(bt, True)
            first_attention(BATCH - 1, False)
            dve.wait_ge(S["a_y"], TILES)
            V.memset(wkT[:, 0, :, 0:WINDOW], 0.0).then_inc(S["dve_step"], 1)
            V.memset(wvs[0:WINDOW, 0, :], 0.0).then_inc(S["dve_step"], 1)
            dve.wait_ge(S["dve_step"], 2)
            dve.sem_inc(S["stream"], 1)
            D0 = 2
            PER = 1 + 1 + TILES + GROUPS
            with dve.Fori(0, DEPTH) as l:
                L0 = D0 + l * PER
                dve.wait_ge(S["consts"], DMA)
                dve.wait_ge(S["wl_ld"], DMA * 20 * (l + 1))
                V.tensor_tensor(tab[:], base[:], qks[:].unsqueeze(1).broadcast_to([P, TPB, 4, DH]),
                                ALU.mult).then_inc(S["dve_step"], 1)
                dve.wait_ge(S["dve_step"], L0 + 1)

                def sumsq(t):
                    G = l * TILES + t
                    dve.wait_ge(S["sq_ok"], 2 * G + 2)
                    V.tensor_reduce(ss[:], sq.rearrange("p (h d) -> p h d", d=DH), AX.X, ALU.add).then_inc(S["ss_sum"], 1)
                    dve.wait_ge(S["ss_sum"], G + 1)
                    V.tensor_scalar(ss[:], ss[:], NORM_MIN2, None, ALU.max).then_inc(S["ss_ok"], 1)

                def rotate(t, first):
                    G = l * TILES + t
                    if not first:
                        dve.wait_ge(S["rot_sum"], G)
                    i = (t & (TPB - 1)) if not isinstance(t, int) else t % TPB
                    def split(a):
                        return a.rearrange("p (s h d) -> p s h d", s=2, d=DH)
                    tb = tab[:, bass.ds(i, 1), :, :].rearrange("p a s d -> p (a s) d")
                    qk = PS[:, 0:2 * BANK]
                    V.tensor_tensor(split(termA), split(qk), tb[:, 0:2, :].unsqueeze(2).broadcast_to([P, 2, HEADS, DH]), ALU.mult)
                    for h in range(2):
                        o, f = h * HALF, (1 - h) * HALF
                        last = V.tensor_tensor(split(termB)[:, :, :, o:o + HALF], split(qk)[:, :, :, f:f + HALF],
                                               tb[:, 2:4, o:o + HALF].unsqueeze(2).broadcast_to([P, 2, HEADS, HALF]), ALU.mult)
                    last.then_inc(S["rot_terms"], 1)

                def normalize(t, first):
                    G = l * TILES + t
                    dve.wait_ge(S["rot_sum"], G + 1)
                    dve.wait_ge(S["rr_ok"], G + 1)
                    if not first:
                        dve.wait_ge(S["tr_ps"], G)
                    V.tensor_tensor(qk_rot.rearrange("p (h d) -> p h d", d=DH), rsum.rearrange("p (h d) -> p h d", d=DH),
                                    rr[:].unsqueeze(2).broadcast_to([P, 2 * HEADS, DH]), ALU.mult).then_inc(S["qk_ok"], 1)

                def rowmax(t, half):
                    G = l * TILES + t
                    dve.wait_ge(S["sc_ps"], 2 * G + half + 1)
                    V.tensor_reduce(wnegmax[:, 4 * half:4 * half + 4], bank(3 + half).rearrange("p (h c) -> p h c", c=P),
                                    AX.X, ALU.max, negate=True).then_inc(S["nm_ok"], 1)

                def pt_evac(t):
                    dve.wait_ge(S["pt_ps"], 2 * (l * TILES + t) + 2)
                    V.tensor_copy(wpT[:, 4:8, :], bank(4).rearrange("p (h c) -> p h c", c=P)).then_inc(S["pt_v"], 1)

                def o_norm(t, u):
                    G = l * TILES + t
                    dve.wait_ge(S["probs"], 2 * G + 2)
                    V.reciprocal(wrinv[:], wrowsum[:, u, :]).then_inc(S["dve_step"], 1)
                    dve.wait_ge(S["dve_step"], L0 + 1 + t + 1)
                    dve.wait_ge(S["o_ps"], G + 1)
                    V.tensor_tensor(o_n.rearrange("p (h d) -> p h d", d=DH), bank(7).rearrange("p (h d) -> p h d", d=DH),
                                    wrinv[:].unsqueeze(2).broadcast_to([P, HEADS, DH]), ALU.mult).then_inc(S["o_ok"], 1)

                def residual(t):
                    G = l * TILES + t
                    dve.wait_ge(S["wo_ps"], G + 1)
                    yt = ys[:, bass.ds(yslot(t), 1), :].rearrange("p a c -> p (a c)")
                    V.tensor_tensor(yt, yt, bank(7, DIM), ALU.add).then_inc(S["updated"], 1)

                def slot(t, u, before=True, after=2):
                    rowmax(t, 0)
                    rowmax(t, 1)
                    if after >= 1:
                        normalize(t + 1, False)
                    if after >= 2:
                        sumsq(t + 2)
                    pt_evac(t)
                    if before:
                        residual(t - 1)
                    if after >= 2:
                        rotate(t + 2, False)
                    o_norm(t, u)

                sumsq(0)
                rotate(0, True)
                normalize(0, True)
                sumsq(1)
                rotate(1, False)
                slot(0, 0, before=False)
                with dve.Fori(0, TILES // 2 - 2) as p:
                    slot(2 * p + 1, 1)
                    slot(2 * p + 2, 0)
                slot(TILES - 3, 1)
                slot(TILES - 2, 0, after=1)
                slot(TILES - 1, 1, after=0)
                residual(TILES - 1)
                dve.wait_ge(S["updated"], (l + 1) * TILES)
                for gu in range(2):
                    last = V.memset(hid[64:P, gu * NB + NB - 1, :], 1.0)
                last.then_inc(S["dve_step"], 1)
                dve.wait_ge(S["dve_step"], L0 + 1 + TILES + 1)
                dve.sem_inc(S["stream"], 1)

                C0 = L0 + 1 + TILES + 1

                def group_stats(g, gu):
                    wait_then_go(*group_loaded(l, g, gu))
                    stats(fmv, fst, lambda i: hc[:, gu, i, :], GT, C0 + g).then_inc(S["c_mv"], 1)

                def group_norm(g, gu):
                    dve.wait_ge(S["c_rs"], l * GROUPS + g + 1)
                    for i in range(GT):
                        last = V.tensor_scalar(hc[:, gu, i, :], hc[:, gu, i, :], fmv[:, i, 0:1], frs[:, i:i + 1],
                                               ALU.subtract, ALU.mult)
                    last.then_inc(S["c_hn"], 1)

                def gate(g, gu, m):
                    o, n = HBLK[m]
                    dve.wait_ge(S["c_gel"], NB * (l * GROUPS + g) + m + 1)
                    V.scalar_tensor_tensor(out=hid[0:n, gu * NB + m, :], in0=bank(2 + m)[0:n], scalar=b_1[0:n, 0, m:m + 1],
                                           in1=gel[0:n, m, :], op0=ALU.add, op1=ALU.mult).then_inc(S["c_hid"], 1)

                def group_residual(g, gu, end=False):
                    G = l * GROUPS + g
                    dve.wait_ge(S["c_out_ps"], G + 1)
                    if not end:
                        dve.wait_ge(*group_loaded(l, g + 1, 1 - gu))
                    s = (g >> 1) * (TPB + 1) + 1 + gu * GT
                    if not isinstance(g, int):
                        s = bounded(s, 1, BATCH * (TPB + 1) - GT)
                    yg = ys[:, bass.ds(s, GT), :]
                    V.tensor_tensor(yg, yg, bank(gu).rearrange("p (i c) -> p i c", c=DIM), ALU.add).then_inc(S["c_out_free"], 1)

                def gslot(g, gu, first=False, last=False):
                    if not last:
                        group_stats(g + 1, 1 - gu)
                    gate(g, gu, 0)
                    if not last:
                        group_norm(g + 1, 1 - gu)
                    gate(g, gu, 1)
                    gate(g, gu, 2)
                    if not first:
                        group_residual(g - 1, 1 - gu)

                group_stats(0, 0)
                group_norm(0, 0)
                gslot(0, 0, first=True)
                with dve.Fori(0, GROUPS // 2 - 1) as p:
                    gslot(2 * p + 1, 1)
                    gslot(2 * p + 2, 0)
                gslot(GROUPS - 1, 1, last=True)
                group_residual(GROUPS - 1, 1, end=True)
                dve.wait_ge(S["c_out_free"], 2 + (l + 1) * GROUPS)
                dve.sem_inc(S["stream"], 1)

            E0 = D0 + DEPTH * PER
            for n in range(BATCH):
                yv = lambda i: ys[:, n * (TPB + 1) + 1 + i, :]
                stats(mv, st, yv, TPB, E0 + 2 * n).then_inc(S["d_mv"], 1)
                dve.wait_ge(S["d_rs"], n + 1)
                if n >= 2:
                    dve.wait_ge(S[f"d_st{n % 2}"], DMA * (n // 2))
                for i in range(TPB):
                    last = V.tensor_scalar(res[:, n % 2, i, :], yv(i), mv[:, i, 0:1], rstd[:, i:i + 1],
                                           ALU.subtract, ALU.mult)
                last.then_inc(S["dve_step"], 1)
                dve.wait_ge(S["dve_step"], E0 + 2 * n + 2)
                V.tensor_tensor(res[:, n % 2], res[:, n % 2], xs[:, n * TPB:(n + 1) * TPB, :], ALU.add).then_inc(S["d_nrm"], 1)

        @block.tensor
        def _(pe):
            pe.wait_ge(S["zeroed"], 5)
            pe.wait_ge(S["w_in_ld"], 3 * DMA)
            with pe.Fori(0, BATCH) as bt:
                pe.wait_ge(S["a_xn"], bt + 1)
                for i in range(TPB):
                    last = tr(bank(i // 4, P, (i % 4) * P), xn[:, i, :], ident[:])
                    if i % 4 == 3:
                        last.then_inc(S["a_xt_ps"], 1)
                pe.wait_ge(S["a_xt"], 2 * bt + 2)
                for j in range(2):
                    mm(bank(2 + j), w_in[:, 0:DIM], xT[:, j * BANK:(j + 1) * BANK], start=True, stop=True).then_inc(S["a_q_ps"], 1)
                for j in range(2):
                    mm(bank(4 + j), w_in[:, DIM:2 * DIM], xT[:, j * BANK:(j + 1) * BANK], start=True, stop=True).then_inc(S["a_k_ps"], 1)
                for i in range(TPB):
                    last = mm(bank(6 + i // 4, DIM, (i % 4) * DIM), xT[:, i * P:(i + 1) * P], w_in[:, 2 * DIM:3 * DIM],
                              start=True, stop=True)
                    if i % 4 == 3:
                        last.then_inc(S["a_v_ps"], 1)
                pe.wait_ge(S["a_qT"], 2 * bt + 2)
                pe.wait_ge(S["a_kT"], 2 * bt + 2)

                def scores(i):
                    if i >= 2:
                        pe.wait_ge(S["a_exp"], bt * TPB + i - 1)
                    n = (i + 1) * P
                    for c in range(0, n, BANK):
                        w = min(BANK, n - c)
                        o = PS[:, (i % 2) * 2 * BANK + c:(i % 2) * 2 * BANK + c + w]
                        last = mm(o, qT[:, i * P:(i + 1) * P], kT[:, c:c + w], start=True, stop=c + w < n)
                    o = PS[:, (i % 2) * 2 * BANK + i * P:(i % 2) * 2 * BANK + n]
                    mm(o, identb[:], causal[:], start=False, stop=True).then_inc(S["a_sc"], 1)

                scores(0)
                pe.wait_ge(S["a_v"], 2 * bt + 2)
                for i in range(TPB):
                    if i + 1 < TPB:
                        scores(i + 1)
                    pe.wait_ge(S["a_exp"], bt * TPB + i + 1)
                    for j in range(i + 1):
                        last = tr(bank(4 + j // 4, P, (j % 4) * P), prob[:, i % 2, j * P:(j + 1) * P], ident[:])
                    last.then_inc(S["a_pt"], 1)
                    pe.wait_ge(S["a_pt_a"], bt * TPB + i + 1)
                    if i >= 4:
                        pe.wait_ge(S["a_pt_v"], bt * 4 + i - 3)
                    if i >= 2:
                        pe.wait_ge(S["a_o"], bt * TPB + i - 1)
                    for j in range(i + 1):
                        last = mm(bank(6 + i % 2, DIM), pT[:, j * P:(j + 1) * P], v_sb[:, j, :], start=(j == 0), stop=(j == i))
                    last.then_inc(S["a_pv"], 1)

            with pe.Fori(0, DEPTH) as l:
                pe.wait_ge(S["stream"], 2 * l + 1)
                pe.wait_ge(S["wl_ld"], DMA * 20 * (l + 1))

                def xt(t, u, first):
                    G = l * TILES + t
                    pe.wait_ge(*h_loaded(l, t, u))
                    if not first:
                        pe.wait_ge(S["v_ok"], G)
                    tr(bank(2, P), h_in[:, u, :], ident[:]).then_inc(S["xt_ps"], 1)

                def qkv(t, first):
                    G = l * TILES + t
                    pe.wait_ge(S["h_t"], G + 1)
                    if not first:
                        pe.wait_ge(S["rot_terms"], G)
                    mm(bank(0), hT, w_qkv[:, 0:INNER], start=True, stop=True).then_inc(S["q_ps"], 1)
                    mm(bank(1), hT, w_qkv[:, INNER:2 * INNER], start=True, stop=True).then_inc(S["k_ps"], 1)
                    mm(bank(2), hT, w_qkv[:, 2 * INNER:], start=True, stop=True).then_inc(S["v_ps"], 1)

                def turn_qk(t, before):
                    pe.wait_ge(S["qk_ok"], l * TILES + t + 1)
                    if before:
                        pe.wait_ge(S["ot_ok"], l * TILES + t - 1)
                    for c in range(2 * INNER // P):
                        last = tr(bank(5 + c // 4, P, (c % 4) * P), qk_rot[:, c * P:(c + 1) * P], ident[:])
                    last.then_inc(S["tr_ps"], 1)

                def turn_probs(t, half):
                    pe.wait_ge(S["probs"], 2 * (l * TILES + t) + half + 1)
                    for j in range(half * 4, half * 4 + 4):
                        last = tr(bank(3 + half, P, (j % 4) * P), wprob[:, j, :], ident[:])
                    last.then_inc(S["pt_ps"], 1)

                def values(t, u, before):
                    G = l * TILES + t
                    pe.wait_ge(S["pt_a"], G + 1)
                    pe.wait_ge(S["pt_v"], G + 1)
                    pe.wait_ge(*hi_shifted(l, t, u))
                    if before:
                        pe.wait_ge(*lo_shifted(l, t - 1, 1 - u))
                        pe.wait_ge(S["updated"], G)
                    for j in range(HEADS):
                        h = head(j)
                        c = slice(h * DH, (h + 1) * DH)
                        mm(bank(7, DH, h * DH)[0:WINDOW], wpT[:, j, 0:WINDOW], wvs[:, u, c], start=True, stop=True)
                        last = mm(bank(7, DH, h * DH)[WINDOW:P], wpT[:, j, WINDOW:P], wv[:, u, c], start=True, stop=True)
                    last.then_inc(S["o_ps"], 1)

                def wscores(t, u, half):
                    G = l * TILES + t
                    pe.wait_ge(S["qk_t"], G + 1)
                    if isinstance(t, int):
                        msk = band[:, 0 if t % TPB == 0 else 1, :]
                    else:
                        sel = bounded(((t & (TPB - 1)) + (TPB - 1)) >> 3, 0, 1)
                        msk = band[:, bass.ds(sel, 1), :].rearrange("p a c -> p (a c)")
                    mm(bank(3 + half), identb[:], msk, start=True, stop=False)
                    for j in range(half * 4, half * 4 + 4):
                        h = head(j)
                        r, g = slice((h % 2) * DH, (h % 2 + 1) * DH), h // 2
                        o = bank(3 + half, P, (j % 4) * P)
                        mm(o[0:WINDOW], wqT[r, g, 0:WINDOW], wkT[r, u, g, 0:P], start=False, stop=(j % 4 == 3))
                        last = mm(o[WINDOW:P], wqT[r, g, WINDOW:P], wkT[r, u, g, WINDOW:], start=False, stop=(j % 4 == 3))
                    last.then_inc(S["sc_ps"], 1)

                def turn_o(t):
                    pe.wait_ge(S["o_ok"], l * TILES + t + 1)
                    for c in range(INNER // P):
                        last = tr(bank(5, P, c * P), o_n[:, c * P:(c + 1) * P], ident[:])
                    last.then_inc(S["ot_ps"], 1)

                def project(t):
                    pe.wait_ge(S["ot_ok"], l * TILES + t + 1)
                    for c in range(INNER // P):
                        last = mm(bank(7, DIM), oT[:, c, :], w_o[:, c, :], start=(c == 0), stop=(c == INNER // P - 1))
                    last.then_inc(S["wo_ps"], 1)

                def slot(t, u, before=True, after=2):
                    wscores(t, u, 0)
                    if after >= 2:
                        xt(t + 2, u, False)
                    wscores(t, u, 1)
                    if before:
                        turn_o(t - 1)
                    if after >= 2:
                        qkv(t + 2, False)
                    turn_probs(t, 0)
                    if after >= 1:
                        turn_qk(t + 1, before)
                    turn_probs(t, 1)
                    if before:
                        project(t - 1)
                    values(t, u, before)

                xt(0, 0, True)
                qkv(0, True)
                xt(1, 1, False)
                turn_qk(0, False)
                qkv(1, False)
                slot(0, 0, before=False)
                with pe.Fori(0, TILES // 2 - 2) as p:
                    slot(2 * p + 1, 1)
                    slot(2 * p + 2, 0)
                slot(TILES - 3, 1)
                slot(TILES - 2, 0, after=1)
                slot(TILES - 1, 1, after=0)
                turn_o(TILES - 1)
                project(TILES - 1)

                pe.wait_ge(S["stream"], 2 * l + 2)

                def turn_h(g, gu, first=False):
                    G = l * GROUPS + g
                    pe.wait_ge(S["c_hn"], G + 1)
                    if not first:
                        pe.wait_ge(S["c_hid"], NB * (G - 1) + 1)
                    for i in range(GT):
                        last = tr(bank(2, P, i * P), hc[:, gu, i, :], ident[:])
                    last.then_inc(S["c_t_ps"], 1)

                def up(g, gu, first=False):
                    G = l * GROUPS + g
                    pe.wait_ge(S["c_hT"], G + 1)
                    for m, (o, n) in enumerate(HBLK):
                        if not first:
                            pe.wait_ge(S["c_hid"], NB * (G - 1) + m + 1)
                        mm(bank(2 + m)[0:n], w_1[:, o:o + n], hcT, start=True, stop=True)
                        mm(bank(5 + m)[0:n], w_1[:, HID + o:HID + o + n], hcT, start=True, stop=True).then_inc(S["c_g_ps"], 1)

                def down(g, gu, half):
                    G = l * GROUPS + g
                    if half == 0:
                        pe.wait_ge(S["c_hid"], NB * (G + 1))
                        pe.wait_ge(S["c_out_free"], G + 1)
                    for i in range(2 * half, 2 * half + 2):
                        for m, (o, n) in enumerate(HBLK):
                            n += m == NB - 1
                            last = mm(bank(gu, DIM, i * DIM), hid[0:n, gu * NB + m, i * P:(i + 1) * P], w_2[0:n, m, :],
                                      start=(m == 0), stop=(m == NB - 1))
                    if half:
                        last.then_inc(S["c_out_ps"], 1)

                def gslot(g, gu, first=False, last=False):
                    up(g, gu, first)
                    if not first:
                        down(g - 1, 1 - gu, 0)
                    if not last:
                        turn_h(g + 1, 1 - gu)
                    if not first:
                        down(g - 1, 1 - gu, 1)

                turn_h(0, 0, first=True)
                gslot(0, 0, first=True)
                with pe.Fori(0, GROUPS // 2 - 1) as p:
                    gslot(2 * p + 1, 1)
                    gslot(2 * p + 2, 0)
                gslot(GROUPS - 1, 1, last=True)
                down(GROUPS - 1, 1, 0)
                down(GROUPS - 1, 1, 1)


_INS = ['L0_attn_x', 'L0_attn_W', 'L0_attn_b', 'L0_ffn_wqkv', 'L0_ffn_q_scale', 'L0_ffn_k_scale', 'L0_ffn_wo',
        'L0_ffn_ln_g', 'L0_ffn_ln_b', 'L0_ffn_w1', 'L0_ffn_b1', 'L0_ffn_w2', 'L0_ffn_b2']


def xpos_tables():
    import numpy as np
    f = np.float32
    half_idx = np.arange(0, DH, 2, dtype=f)
    inv_freq = (f(1.0) / np.power(f(10000.0), half_idx / f(DH))).astype(f)
    t = np.arange(SEQ, dtype=f)
    freqs = t[:, None] * inv_freq[None, :]
    base = (half_idx + f(0.4 * DH)) / f(1.4 * DH)
    power = (t - f(SEQ // 2)) / f(WINDOW // 2)
    scale = np.power(base[None, :], power[:, None]).astype(f)
    cos, sin = np.cos(freqs).astype(f), np.sin(freqs).astype(f)
    q8 = f(QK_SCALE)
    rows = [np.concatenate([cos * scale * q8] * 2, -1), np.concatenate([cos / scale] * 2, -1),
            np.concatenate([-sin * scale * q8, sin * scale * q8], -1), np.concatenate([-sin / scale, sin / scale], -1)]
    tab = np.stack(rows, 1).astype(f)
    return np.ascontiguousarray(tab.reshape(TPB, P, 4, DH).transpose(1, 0, 2, 3))


def kernel(**inputs):
    import numpy as _np
    import concourse.bacc as _bacc
    from concourse.bass_utils import run_bass_kernel_spmd as _run

    nc = _bacc.Bacc("TRN2", target_bir_lowering=False, num_devices=1)
    arrays, args = {}, []
    for name in _INS:
        a = _np.ascontiguousarray(inputs[name])
        arrays[f"in_{name}"] = a
        args.append(nc.dram_tensor(f"in_{name}", a.shape, mybir.dt.from_np(a.dtype), kind="ExternalInput").ap())
    tables = xpos_tables()
    arrays["xpos"] = tables
    args.append(nc.dram_tensor("xpos", tables.shape, mybir.dt.from_np(tables.dtype), kind="ExternalInput").ap())
    out = nc.dram_tensor("out_0", (BATCH, SEQ, DIM), mybir.dt.float32, kind="ExternalOutput").ap()
    build_program(nc, *args, out)
    r = _run(nc, [arrays], core_ids=[0])
    return r.results[0]["out_0"]
```

```python
import concourse.bass as bass
from concourse import mybir
from contextlib import ExitStack

P = 128
BATCH = 8
SEQ = 1024
DIM = 128
TPB = SEQ // P
TILES = BATCH * TPB
DEPTH = 2
HEADS = 8
DH = 64
INNER = HEADS * DH
WINDOW = 64
HALF = DH // 2
HID = int(DIM * 4 * 2 / 3)
HBLK = [(0, P), (P, P), (2 * P, HID - 2 * P)]
NB = len(HBLK)
TAIL = HBLK[-1][1]
GT = 4
GROUPS = TILES // GT
BANK = 512
SLOTS = TILES + 2
LN_EPS = 1e-5
NORM_MIN2 = 1e-24
ATT_SCALE = float(DIM) ** -0.5
QK_SCALE = 8.0
NEG = -3.0e38
WA_LOADS, WF_LOADS = 8, 12
DMA = 16
LAST_DVE = 5 * DIM
REGION = 13824


def build_program(nc, x, W, b, wqkv, q_scale, k_scale, wo, ln_g, ln_b, w1, b1, w2, b2, xpos, out):
    f32, bf16 = mybir.dt.float32, mybir.dt.bfloat16
    f32r = mybir.dt.float32r
    ALU, ACT, AX = mybir.AluOpType, mybir.ActivationFunctionType, mybir.AxisListType
    mm, tr = nc.tensor.matmul, nc.tensor.transpose

    with ExitStack() as ctx:
        def sb(name, shape, dt=f32):
            return ctx.enter_context(nc.sbuf_tensor(name, shape, dt))

        def sem(name):
            return ctx.enter_context(nc.semaphore(name))

        xs = sb("xs", [P, TILES, DIM])
        ys = sb("ys", [P, BATCH * (TPB + 1), DIM])
        ident = sb("ident", [P, P])
        identb = sb("identb", [P, P], bf16)
        causal = sb("causal", [P, P], bf16)
        band = sb("band", [P, 2, BANK], bf16)
        carrier = sb("carrier", [P, 2])
        eps = sb("eps", [P, TPB])
        warm = sb("warm", [P, 1])
        half_neg = sb("half_neg", [P, 2 * HEADS])
        w_in = sb("w_in", [P, 3 * DIM])
        b_col = sb("b_col", [P, 2])
        bv_all = sb("bv_all", [P, DIM])
        region = sb("region", [P, REGION])
        used = [0]

        def part(*shape):
            n = 1
            for s in shape:
                n *= s
            v = region[:, used[0]:used[0] + n]
            used[0] += n
            assert used[0] <= REGION, used[0]
            if len(shape) == 2:
                v = v.rearrange("p (a b) -> p a b", a=shape[0])
            if len(shape) == 3:
                v = v.rearrange("p (a b c) -> p a b c", a=shape[0], b=shape[1])
            return v

        st = sb("st", [P, TPB, 6])
        mv = sb("mv", [P, TPB, 2])
        rstd = sb("rstd", [P, TPB])

        xn = part(TPB, DIM)
        xT = part(SEQ)
        qT = part(2, SEQ)
        kT = part(2, SEQ)
        v_sb = part(2, TPB * DIM)
        prob = part(2, SEQ)
        pT = part(SEQ)
        o_sb = part(TPB, DIM)
        negmax = sb("negmax", [P, 2])
        rowsum = sb("rowsum", [P, 2])
        rinv = sb("rinv", [P, 2])
        O, N, Y = 0, 1, 2
        st3 = sb("st3", [P, 2, 3, 6])
        mv3 = sb("mv3", [P, 2, 3, 2])
        rstd3 = sb("rstd3", [P, 2, 3])
        nmean3 = sb("nmean3", [P, 2, 3])
        neg_one = sb("neg_one", [P, TPB])

        used[0] = 0
        w_qkv = sb("w_qkv", [P, 3 * INNER])
        w_o = sb("w_o", [P, INNER // P, DIM])
        base = sb("base", [P, TPB, 4, DH])
        tab = sb("tab", [P, TPB, 4, DH])
        qks = sb("qks", [P, 4, DH])
        w_qkv_hi = sb("w_qkv_hi", [P, 3 * INNER], f32r)
        w_qkv_lo = sb("w_qkv_lo", [P, 3 * INNER], f32r)
        hT_hi = sb("hT_hi", [P, P], f32r)
        hT_lo = sb("hT_lo", [P, P], f32r)
        h_in = part(2, DIM)
        sq = part(2 * INNER)
        termA = part(2 * INNER)
        termB = part(2 * INNER)
        rsum = part(2 * INNER)
        qk_rot = part(2 * INNER)
        wqT = part(HEADS // 2, P)
        wkT = part(2, HEADS // 2, P + WINDOW)
        wv = part(4, INNER)
        wvs = part(2, INNER)
        wprob = part(HEADS, P)
        wpT = part(HEADS, P)
        oT = part(HEADS // 2, P)
        ss = sb("ss", [P, 2 * HEADS])
        rr = sb("rr", [P, 2 * HEADS])
        wnegmax = sb("wnegmax", [P, HEADS])
        wrowsum = sb("wrowsum", [P, 2, HEADS])
        wrinv = sb("wrinv", [P, HEADS])

        used[0] = 2 * DIM
        hc = part(2, GT, DIM)
        hid_tail = part(2, GT * P)
        hcT = part(GT * P)
        w_1 = sb("w_1", [P, 2 * HID])
        w_2 = sb("w_2", [P, NB, DIM])
        w_1_hi = sb("w_1_hi", [P, 2 * HID], f32r)
        w_1_lo = sb("w_1_lo", [P, 2 * HID], f32r)
        hcT_hi = sb("hcT_hi", [P, GT * P], f32r)
        hcT_lo = sb("hcT_lo", [P, GT * P], f32r)
        b_1 = sb("b_1", [P, 2, NB])
        ln_cols = sb("ln_cols", [P, 2])
        used[0] = 6 * SEQ
        gel = part(NB, GT * P)
        hid = part(2 * (NB - 1), GT * P)
        fst = sb("fst", [P, GT, 6])
        fmv = sb("fmv", [P, GT, 2])
        frs = sb("frs", [P, GT])
        used[0] = 0
        res = part(BATCH, SEQ)
        st2 = part(BATCH, TPB, 6)
        mv2 = part(BATCH, TPB, 2)
        rstd2 = part(BATCH, TPB)
        nmr2 = part(BATCH, TPB)

        PS = ctx.enter_context(nc.psum_tensor("PS", [P, 8 * BANK], f32))

        def bank(n, cols=BANK, off=0):
            return PS[:, n * BANK + off:n * BANK + off + cols]

        names = """consts iota0 h_go w_in_ld wa_ld wf_ld x_ld zeroed n_step n_mv n_rstd ln_step ln_mv ln_rs x1_step a_xn ch_ps
            ch_a ch_v a_sc a_nm a_exp a_pt a_pt_a a_pt_v a_pv a_o a_oap a_bcol dve_step pool_step stream h_ld0
            h_ld1 xt_ps h_hi h_t wa_hi wa_lo wf_hi wf_lo tab_ok q_ps k_ps v_ps sq_ok ss_sum ss_ok rr_ok
            rot_terms rot_sum qk_ok qk_t sc_ps nm_ok probs pt_ps pt_ok rinv_ok pn_ok v_ok vs_hi0 vs_hi1 vs_lo0
            vs_lo1 o_ps ot_ok wo_ps q_turned k_turned hc_ld0 hc_ld1 c_step c_mv c_rs c_hn c_t_ps c_hT c_hi c_lo
            c_g_ps c_gel c_hid c_out_ps c_out_free d_mv d_rs d_app d_nrm d_pool stored a_y a_rinv updated ones""".split()
        S = {n: sem(n) for n in names}

        def head(j):
            return 2 * (j % (HEADS // 2)) + j // (HEADS // 2)

        def h_loaded(l, t, u):
            return S[f"h_ld{u}"], 3 * DMA * (l * (TILES // 2) + (t >> 1) + 1)

        def hi_shifted(l, t, u):
            return S[f"vs_hi{u}"], DMA * (l * (TILES // 2) + (t >> 1) + 1)

        def lo_shifted(l, t, u):
            return S[f"vs_lo{u}"], DMA * (l * (TILES // 2 - u) + (t >> 1) + 1)

        def group_loaded(l, g, u):
            return S[f"hc_ld{u}"], 3 * DMA * (l * (GROUPS // 2) + (g >> 1) + 1)

        def hidden(gu, m):
            return hid_tail[:, gu] if m == NB - 1 else hid[:, gu * (NB - 1) + m]

        def bounded(v, low, high):
            return v.with_bounds(min_val=low, max_val=high)

        def yslot(t):
            if isinstance(t, int):
                return t + t // TPB + 1
            return bounded(t + (t >> 3) + 1, 1, BATCH * (TPB + 1) - 1)

        block = ctx.enter_context(nc.Block())
        x_t = x.rearrange("b (i p) c -> b p i c", p=P)
        out_t = out.rearrange("b (i p) c -> b p i c", p=P)

        @block.sync
        def _(sp):
            sp.dma_start(w_in[:], W).then_inc(S["w_in_ld"], DMA)
            sp.dma_start(b_col[:], b[0:2 * DIM].rearrange("(s c) -> c s", s=2),
                         allow_slow_non_contiguous=True).then_inc(S["w_in_ld"], DMA)
            sp.dma_start(bv_all[:], b[2 * DIM:3 * DIM].partition_broadcast(P)).then_inc(S["w_in_ld"], DMA)

            def load(done, pairs):
                for dst, src in pairs:
                    sp.dma_start(dst, src, allow_slow_non_contiguous=True).then_inc(S[done], DMA)

            def load_attention_weights(l):
                at = bass.ds(l, 1)
                loads = [(w_qkv[:], wqkv[at].rearrange("a c n -> (a c) n")),
                         (w_o[:], wo[at].rearrange("a (k c) n -> (a c) k n", c=P))]
                for s, scale in enumerate((q_scale, k_scale)):
                    loads.append((qks[:, s, :], scale[at].rearrange("a c -> (a c)").partition_broadcast(P)))
                    for h in range(2):
                        loads.append((qks[:, 2 + s, h * HALF:(h + 1) * HALF], scale[at, (1 - h) * HALF:(2 - h) * HALF]
                                      .rearrange("a c -> (a c)").partition_broadcast(P)))
                assert len(loads) == WA_LOADS
                load("wa_ld", loads)

            def load_ff_weights(l):
                at = bass.ds(l, 1)
                loads = [(w_1[:], w1[at].rearrange("a c n -> (a c) n")),
                         (w_2[:, 0:2, :], w2[at, 0:2 * P].rearrange("a (k c) n -> (a c) k n", c=P)),
                         (w_2[0:TAIL, 2, :], w2[at, 2 * P:HID].rearrange("a c n -> (a c) n")),
                         (w_2[TAIL:TAIL + 1, 2, :], b2[at]),
                         (ln_cols[:, 0:1], ln_g[at].rearrange("a c -> c a")),
                         (ln_cols[:, 1:2], ln_b[at].rearrange("a c -> c a"))]
                for s in range(2):
                    for m, (o, n) in enumerate(HBLK):
                        loads.append((b_1[0:n, s, m:m + 1], b1[at, s * HID + o:s * HID + o + n].rearrange("a c -> c a")))
                assert len(loads) == WF_LOADS
                load("wf_ld", loads)

            for n in range(BATCH):
                if n:
                    sp.wait_ge(S["x_ld"], DMA * n)
                sp.dma_start(xs[:, n * TPB:(n + 1) * TPB, :], x_t[n]).then_inc(S["x_ld"], DMA)
                if n == 0:
                    sp.dma_start(base[:], xpos).then_inc(S["consts"], DMA)
                    load_attention_weights(0)

            def shifted(l, t, u, free=None):
                s = sp.snap(yslot(t)) if free is not None else yslot(t)
                if free is not None:
                    sp.wait_ge(S["xt_ps"], free)
                sp.dma_start(h_in[:, u, 0:DIM // 2], ys[:, bass.ds(s, 1), 0:DIM // 2]).then_inc(S[f"h_ld{u}"], DMA)
                sp.dma_start(h_in[1:P, u, DIM // 2:], ys[0:P - 1, bass.ds(s, 1), DIM // 2:]).then_inc(S[f"h_ld{u}"], DMA)
                sp.dma_start(h_in[0:1, u, DIM // 2:], ys[P - 1:P, bass.ds(s - 1, 1), DIM // 2:]).then_inc(S[f"h_ld{u}"], DMA)

            def v_shift(l, t, k, last=False):
                G, u = l * TILES + t, k % 2
                sp.wait_ge(S["v_ok"], G + 1)
                sp.dma_start(wvs[WINDOW:P, u, :], wv[0:WINDOW, k, :]).then_inc(S[f"vs_hi{u}"], DMA)
                if not last:
                    if not (isinstance(t, int) and t == 0):
                        sp.wait_ge(S["o_ps"], G)
                    sp.dma_start(wvs[0:WINDOW, 1 - u, :], wv[WINDOW:P, k, :]).then_inc(S[f"vs_lo{u}"], DMA)

            def shifted_group(l, bt, gu):
                s = bt * (TPB + 1) + 1 + gu * GT
                sp.dma_start(hc[:, gu, :, 0:DIM // 2], ys[:, bass.ds(s, GT), 0:DIM // 2]).then_inc(S[f"hc_ld{gu}"], DMA)
                sp.dma_start(hc[1:P, gu, :, DIM // 2:], ys[0:P - 1, bass.ds(s, GT), DIM // 2:]).then_inc(S[f"hc_ld{gu}"], DMA)
                sp.dma_start(hc[0:1, gu, :, DIM // 2:], ys[P - 1:P, bass.ds(s - 1, GT), DIM // 2:]).then_inc(S[f"hc_ld{gu}"], DMA)

            with sp.Fori(0, DEPTH) as l:
                following = sp.snap((l + 1) & (DEPTH - 1))
                sp.wait_ge(S["h_go"], l + 1)
                shifted(l, 0, 0)
                shifted(l, 1, 1)
                sp.wait_ge(S["stream"], 2 * l + 1)
                load_ff_weights(l)

                def ahead(t, u):
                    shifted(l, t + 2, u, l * TILES + t + 1)

                ahead(0, 0)
                v_shift(l, 0, 0)
                with sp.Fori(0, TILES // 4 - 1) as p:
                    for k in (1, 2, 3, 4):
                        ahead(4 * p + k, k % 2)
                        v_shift(l, 4 * p + k, k % 4)
                ahead(TILES - 3, 1)
                v_shift(l, TILES - 3, 1)
                v_shift(l, TILES - 2, 2)
                v_shift(l, TILES - 1, 3, last=True)

                sp.wait_ge(S["ss_ok"], (l + 1) * TILES)
                shifted_group(l, 0, 0)
                shifted_group(l, 0, 1)
                def groups_of(bt):
                    for gu in range(2):
                        sp.wait_ge(S["c_t_ps"], l * GROUPS + 2 * bt + gu - 1)
                        shifted_group(l, bt, gu)

                with sp.Fori(1, BATCH - 1) as bt:
                    groups_of(bt)
                load_attention_weights(following)
                groups_of(BATCH - 1)

            for n in range(BATCH):
                sp.wait_ge(S["d_nrm"], n + 1)
                sp.wait_ge(S["d_pool"], n + 1)
                sp.dma_start(out_t[n], res[:, n].rearrange("p (i c) -> p i c", c=DIM)).then_inc(S["stored"], DMA)
            sp.wait_ge(S["stored"], DMA * BATCH)

        @block.gpsimd
        def _(pool):
            pool.memset(ident[:], 0.0).then_inc(S["iota0"], 1)
            pool.memset(causal[:], 0.0).then_inc(S["iota0"], 1)
            pool.memset(band[:], 0.0).then_inc(S["iota0"], 1)
            pool.memset(half_neg[:], -0.5)
            pool.memset(neg_one[:], -1.0)
            pool.memset(mv3[:], 0.0)
            pool.memset(eps[:], LN_EPS).then_inc(S["zeroed"], 1)
            pool.memset(ys[:, :, :].rearrange("p (n i) c -> p n i c", n=BATCH)[:, :, 0, :], 0.0).then_inc(S["zeroed"], 1)
            pool.wait_ge(S["iota0"], 3)
            pool.affine_select(out=ident[:], in_=ident[:], compare_op=ALU.not_equal, fill=1.0, base=0,
                               pattern=[[-1, P]], channel_multiplier=1).then_inc(S["iota0"], 1)
            pool.affine_select(out=causal[:], in_=causal[:], compare_op=ALU.is_ge, fill=NEG, base=0,
                               pattern=[[-1, P]], channel_multiplier=1).then_inc(S["zeroed"], 1)
            n = 4
            for lo in (0, WINDOW):
                rows = band[lo:lo + WINDOW].rearrange("p s (h c) -> p (s h) c", c=P)
                pool.wait_ge(S["iota0"], n)
                pool.affine_select(out=rows, in_=rows, compare_op=ALU.is_ge, fill=NEG, base=0,
                                   pattern=[[0, 2 * BANK // P], [1, P]], channel_multiplier=-1).then_inc(S["iota0"], 1)
                n += 1
                pool.wait_ge(S["iota0"], n)
                pool.affine_select(out=rows, in_=rows, compare_op=ALU.is_ge, fill=NEG, base=WINDOW,
                                   pattern=[[0, 2 * BANK // P], [-1, P]], channel_multiplier=1).then_inc(S["iota0"], 1)
                n += 1
            pool.wait_ge(S["iota0"], n)
            pool.memset(band[0:WINDOW, 0, :].rearrange("p (h c) -> p h c", c=P)[:, :, 0:WINDOW], NEG).then_inc(S["zeroed"], 1)

            def rsqrt(dst, src, wait, done, n):
                pool.wait_ge(S[wait[0]], wait[1])
                pool.tensor_tensor(dst, src, eps[:, 0:n], ALU.add).then_inc(S["pool_step"], 1)
                pool.wait_ge(S["pool_step"], pstep(1))
                pool.tensor_tensor(dst, dst, half_neg[:, 0:n], ALU.pow).then_inc(S[done], 1)

            POOL_A = 2 + 3 * SLOTS

            def pstep(k):
                return pcount[0] + k
            pcount = [0]
            pool.wait_ge(S["zeroed"], 5)

            for n in range(2):
                pcount[0] = n
                rsqrt(rstd[:], mv[:, :, 1], ("n_mv", n + 1), "n_rstd", TPB)

            def slot_norms(s, u, applied):
                r, m, step = rstd3[:, u, :], nmean3[:, u, :], 2 + 3 * s
                if applied is not None:
                    pool.wait_ge(S["a_oap"], applied)
                pool.wait_ge(S["ln_mv"], s + 1)
                pool.tensor_tensor(r, mv3[:, u, :, 1], eps[:, 0:3], ALU.add).then_inc(S["pool_step"], 1)
                pool.tensor_tensor(m, mv3[:, u, :, 0], neg_one[:, 0:3], ALU.mult).then_inc(S["pool_step"], 1)
                pool.wait_ge(S["pool_step"], step + 2)
                pool.tensor_tensor(r, r, half_neg[:, 0:3], ALU.pow).then_inc(S["pool_step"], 1)
                pool.wait_ge(S["pool_step"], step + 3)
                pool.tensor_tensor(m, m, r, ALU.mult).then_inc(S["ln_rs"], 1)

            for s in range(4):
                slot_norms(s, s % 2, s - 2 if s > 2 else None)
            with pool.Fori(2, SLOTS // 2 - 1) as p:
                for u in range(2):
                    slot_norms(2 * p + u, u, 2 * p + u - 2)
            for s in (SLOTS - 2, SLOTS - 1):
                slot_norms(s, s % 2, min(s - 2, TILES))

            with pool.Fori(0, DEPTH) as l:
                def norms(t, first):
                    G = l * TILES + t
                    pool.wait_ge(S["ss_ok"], G + 1)
                    if not first:
                        pool.wait_ge(S["qk_ok"], G)
                    pool.tensor_tensor(rr[:], ss[:], half_neg[:], ALU.pow).then_inc(S["rr_ok"], 1)
                    pool.wait_ge(S["rot_terms"], G + 1)
                    pool.tensor_tensor(rsum[:], termA[:], termB[:], ALU.add).then_inc(S["rot_sum"], 1)

                norms(0, True)
                with pool.Fori(0, TILES // 2 - 1) as p:
                    norms(2 * p + 1, False)
                    norms(2 * p + 2, False)
                norms(TILES - 1, False)
                with pool.Fori(0, GROUPS) as g:
                    pcount[0] = POOL_A + l * GROUPS + g
                    rsqrt(frs[:], fmv[:, :, 1], ("c_mv", l * GROUPS + g + 1), "c_rs", GT)

            for n in range(BATCH + 2):
                if n < BATCH:
                    k = POOL_A + DEPTH * GROUPS + 3 * n
                    r, m = rstd2[:, n], nmr2[:, n]
                    pool.wait_ge(S["d_mv"], n + 1)
                    pool.tensor_tensor(r, mv2[:, n, :, 1], eps[:], ALU.add).then_inc(S["pool_step"], 1)
                    pool.tensor_tensor(m, mv2[:, n, :, 0], neg_one[:], ALU.mult).then_inc(S["pool_step"], 1)
                    pool.wait_ge(S["pool_step"], k + 2)
                    pool.tensor_tensor(r, r, half_neg[:, 0:TPB], ALU.pow).then_inc(S["pool_step"], 1)
                    pool.wait_ge(S["pool_step"], k + 3)
                    pool.tensor_tensor(m, m, r, ALU.mult).then_inc(S["d_rs"], 1)
                if n >= 2:
                    m, c = n - 2, slice(LAST_DVE, SEQ)
                    pool.wait_ge(S["d_app"], m + 1)
                    pool.tensor_tensor(res[:, m, c], res[:, m, c],
                                       xs[:, m * TPB:(m + 1) * TPB, :].rearrange("p i c -> p (i c)")[:, c],
                                       ALU.add).then_inc(S["d_pool"], 1)

        @block.scalar
        def _(act):
            A = act.activation
            act.wait_ge(S["zeroed"], 5)
            A(warm[:], eps[:, 0:1], ACT.Exp)
            act.wait_ge(S["a_bcol"], 1)

            def piece_out(q, u, j, ps):
                act.wait_ge(S["ch_ps"], 8 * q + j + 1)
                c = slice((j % 2) * BANK, (j % 2 + 1) * BANK)
                if j < 2:
                    done = A(xT[:, c], bank(ps), ACT.Copy)
                elif j < 4:
                    done = A(qT[:, u, c], bank(ps), ACT.Identity, bias=b_col[:, 0:1], scale=ATT_SCALE)
                else:
                    done = A(kT[:, u, c], bank(ps), ACT.Identity, bias=b_col[:, 1:2])
                done.then_inc(S["ch_a"], 1)

            def first_exps(g, i):
                n, u = (i + 1) * P, i % 2
                act.wait_ge(S["a_nm"], g + 1)
                A(prob[:, u, 0:n], PS[:, u * 2 * BANK:u * 2 * BANK + n], ACT.Exp,
                  bias=negmax[:, u:u + 1], accum_out=rowsum[:, u:u + 1]).then_inc(S["a_exp"], 1)

            def o_apply(t, i, slot):
                u = (i + 1) % 2
                act.wait_ge(S["ln_rs"], slot)
                A(o_sb[:, i % TPB, :], o_sb[:, i % TPB, :], ACT.Identity, bias=nmean3[:, u, O:O + 1],
                  scale=rstd3[:, u, O:O + 1]).then_inc(S["a_oap"], 1)

            def first_attention(bt, u, first=False, last=False):
                for i in range(TPB):
                    g = bt * TPB + i
                    act.wait_ge(S["a_pt"], g + 1)
                    n = min((i + 1) * P, BANK)
                    A(pT[:, 0:n], bank(4, n), ACT.Copy).then_inc(S["a_pt_a"], 1)
                    if not last and i < 6:
                        piece_out(bt + 1, 1 - u, i, 7)
                    if not (last and i == TPB - 1):
                        first_exps(g + 1, (i + 1) % TPB)
                    if not (first and i < 2):
                        o_apply(g - 2, (i - 2) % TPB, g)
                    act.wait_ge(S["a_rinv"], g + 1)
                    act.wait_ge(S["a_pv"], g + 1)
                    A(o_sb[:, i, :], bank(6, DIM), ACT.Copy, scale=rinv[:, i % 2:i % 2 + 1]).then_inc(S["a_o"], 1)

            for j in range(6):
                piece_out(0, 0, j, j)
            first_exps(0, 0)
            first_attention(0, 0, first=True)
            first_attention(1, 1)
            with act.Fori(1, BATCH // 2 - 1) as p:
                first_attention(2 * p, 0)
                first_attention(2 * p + 1, 1)
            first_attention(BATCH - 2, 0)
            first_attention(BATCH - 1, 1, last=True)
            for t in (TILES - 2, TILES - 1):
                o_apply(t, t % TPB, t + 2)

            with act.Fori(0, DEPTH) as l:

                def h_evac(t):
                    act.wait_ge(S["xt_ps"], l * TILES + t + 1)
                    A(hT_hi[:], bank(2, P), ACT.Copy).then_inc(S["h_hi"], 1)

                def squares(t, first):
                    G = l * TILES + t
                    if not first:
                        act.wait_ge(S["ss_ok"], G)
                    for s, ps in enumerate(("q_ps", "k_ps")):
                        act.wait_ge(S[ps], G + 1)
                        A(sq[:, s * INNER:(s + 1) * INNER], bank(s), ACT.Square).then_inc(S["sq_ok"], 1)

                def v_evac(t, k):
                    G = l * TILES + t
                    act.wait_ge(S["v_ps"], G + 1)
                    if not (isinstance(t, int) and t < 4):
                        act.wait_ge(S["o_ps"], G - 3)
                        act.wait_ge(*hi_shifted(l, t - 4, k % 2))
                        act.wait_ge(*lo_shifted(l, t - 4, k % 2))
                    A(wv[:, k, :], bank(2), ACT.Copy).then_inc(S["v_ok"], 1)

                def exps(t, u, half):
                    G = l * TILES + t
                    act.wait_ge(S["nm_ok"], 2 * G + half + 1)
                    for j in range(half * 4, half * 4 + 4):
                        last = A(wprob[:, j, :], bank(3 + half, P, (j % 4) * P), ACT.Exp,
                                 bias=wnegmax[:, j:j + 1], accum_out=wrowsum[:, u, j:j + 1])
                    last.then_inc(S["probs"], 1)

                def q_evac(t):
                    act.wait_ge(S["q_turned"], l * TILES + t + 1)
                    A(wqT, bank(5), ACT.Copy)

                def k_evac(t, u):
                    act.wait_ge(S["k_turned"], l * TILES + t + 1)
                    kps = bank(6).rearrange("p (g c) -> p g c", c=P)
                    A(wkT[:, u, :, WINDOW:], kps, ACT.Copy)
                    A(wkT[:, 1 - u, :, 0:WINDOW], kps[:, :, P - WINDOW:], ACT.Copy).then_inc(S["qk_t"], 1)

                def pt_evac(t, half):
                    act.wait_ge(S["pt_ps"], 2 * (l * TILES + t) + half + 1)
                    A(wpT[:, 4 * half:4 * half + 4, :], bank(3 + half), ACT.Copy).then_inc(S["pt_ok"], 1)

                def ot_evac(t):
                    act.wait_ge(S["o_ps"], l * TILES + t + 1)
                    A(oT, bank(7), ACT.Copy).then_inc(S["ot_ok"], 1)

                def slot(t, k, before=True, after=2):
                    u = k % 2
                    if before:
                        ot_evac(t - 1)
                    if after >= 2:
                        h_evac(t + 2)
                    exps(t, u, 0)
                    exps(t, u, 1)
                    if after >= 2:
                        squares(t + 2, False)
                    pt_evac(t, 0)
                    if after >= 1:
                        q_evac(t + 1)
                    pt_evac(t, 1)
                    if after >= 1:
                        k_evac(t + 1, 1 - u)
                    if after >= 2:
                        v_evac(t + 2, (k + 2) % 4)

                h_evac(0)
                squares(0, True)
                v_evac(0, 0)
                h_evac(1)
                squares(1, False)
                v_evac(1, 1)
                q_evac(0)
                k_evac(0, 0)
                slot(0, 0, before=False)
                slot(1, 1)
                with act.Fori(0, TILES // 4 - 1) as p:
                    for k in (2, 3, 4, 5):
                        slot(4 * p + k, k % 4)
                slot(TILES - 2, 2, after=1)
                slot(TILES - 1, 3, after=0)

                def hT_evac(g):
                    act.wait_ge(S["c_t_ps"], l * GROUPS + g + 1)
                    A(hcT, bank(2), ACT.Identity, bias=ln_cols[:, 1:2], scale=ln_cols[:, 0:1]).then_inc(S["c_hT"], 1)
                    act.wait_ge(S["c_hT"], l * GROUPS + g + 1)
                    A(hcT_hi[:], hcT, ACT.Copy).then_inc(S["c_hi"], 1)

                def gelus(g, blocks):
                    for m in blocks:
                        o, n = HBLK[m]
                        act.wait_ge(S["c_g_ps"], NB * (l * GROUPS + g) + m + 1)
                        A(gel[0:n, m, :], bank(5 + m)[0:n], ACT.Gelu, bias=b_1[0:n, 1, m:m + 1]).then_inc(S["c_gel"], 1)

                act.wait_ge(S["wf_ld"], DMA * WF_LOADS * (l + 1))
                hT_evac(0)
                ot_evac(TILES - 1)
                gelus(0, range(NB))
                with act.Fori(1, GROUPS) as g:
                    hT_evac(g)
                    gelus(g, range(NB))

            act.wait_ge(S["stream"], 2 * DEPTH + 1)
            for n in range(BATCH):
                act.wait_ge(S["d_rs"], n + 1)
                for i in range(TPB):
                    last = A(res[:, n, i * DIM:(i + 1) * DIM], ys[:, n * (TPB + 1) + 1 + i, :], ACT.Identity,
                             bias=nmr2[:, n, i:i + 1], scale=rstd2[:, n, i:i + 1])
                last.then_inc(S["d_app"], 1)

        @block.vector
        def _(dve):
            V = nc.vector

            def wait_then_go(semaphore, value, k=0):
                dve.wait_ge(semaphore, value)
                V.memset(carrier[:, k:k + 1], 0.0)

            def stats(dst_mv, dst_st, tiles, n, base_count, s="c_step"):
                for i in range(n):
                    last = V.bn_stats(dst_st[:, i, :], tiles(i))
                last.then_inc(S[s], 1)
                wait_then_go(S[s], base_count + 1)
                for i in range(n):
                    last = V.bn_aggr(dst_mv[:, i, :], dst_st[:, i, :])
                return last

            dve.sem_inc(S["c_out_free"], 2)
            dve.wait_ge(S["w_in_ld"], 3 * DMA)
            V.tensor_scalar(b_col[:, 0:1], b_col[:, 0:1], ATT_SCALE, None, ALU.mult).then_inc(S["a_bcol"], 1)
            dve.wait_ge(S["iota0"], 4)
            V.tensor_copy(identb[:], ident[:]).then_inc(S["zeroed"], 1)
            dve.wait_ge(S["zeroed"], 5)
            xt_ = lambda bt, i: xs[:, bass.ds(bt * TPB + i, 1), :].rearrange("p a c -> p (a c)")
            yt_ = lambda bt, i: ys[:, bass.ds(bt * (TPB + 1) + 1 + i, 1), :].rearrange("p a c -> p (a c)")

            def v_out(q, u, j, ps):
                dve.wait_ge(S["ch_ps"], 8 * q + 7 + j)
                V.tensor_tensor(v_sb[:, u, j * BANK:(j + 1) * BANK].rearrange("p (i c) -> p i c", c=DIM),
                                bank(ps).rearrange("p (i c) -> p i c", c=DIM),
                                bv_all[:].unsqueeze(1).broadcast_to([P, 4, DIM]), ALU.add).then_inc(S["ch_v"], 1)

            def sequence_stats(n):
                dve.wait_ge(S["x_ld"], DMA * (n + 1))
                stats(mv, st, lambda i: xs[:, n * TPB + i, :], TPB, n, "n_step").then_inc(S["n_mv"], 1)

            def sequence_norm(n):
                dve.wait_ge(S["n_rstd"], n + 1)
                for i in range(TPB):
                    if n and i in (0, 4):
                        dve.wait_ge(S["ch_ps"], 1 + i // 4)
                    V.tensor_scalar(xn[:, i, :], xs[:, n * TPB + i, :], mv[:, i, 0:1], rstd[:, i:i + 1],
                                    ALU.subtract, ALU.mult).then_inc(S["a_xn"], 1)

            sequence_stats(0)
            sequence_norm(0)
            sequence_stats(1)

            def attention_weights_high(n):
                dve.wait_ge(S["wa_ld"], DMA * WA_LOADS * (n + 1))
                V.tensor_copy(w_qkv_hi[:], w_qkv[:]).then_inc(S["wa_hi"], 1)

            def rotation_tables():
                V.tensor_tensor(tab[:], base[:], qks[:].unsqueeze(1).broadcast_to([P, TPB, 4, DH]),
                                ALU.mult).then_inc(S["tab_ok"], 1)

            def attention_weights_low(n):
                dve.wait_ge(S["wa_hi"], n + 1)
                V.tensor_tensor(w_qkv_lo[:], w_qkv[:], w_qkv_hi[:].bitcast(f32), ALU.subtract).then_inc(S["wa_lo"], 1)


            sequence_norm(1)
            for j in range(2):
                v_out(0, 0, j, 6 + j)

            def first_rowmax(g, i):
                dve.wait_ge(S["a_sc"], g + 1)
                V.tensor_reduce(negmax[:, i % 2:i % 2 + 1],
                                PS[:, (i % 2) * 2 * BANK:(i % 2) * 2 * BANK + (i + 1) * P], AX.X, ALU.max,
                                negate=True).then_inc(S["a_nm"], 1)

            def x1_sum(bt, i, t):
                dve.wait_ge(S["a_oap"], t + 1)
                V.tensor_tensor(xt_(bt, i), xt_(bt, i), o_sb[:, i, :], ALU.add).then_inc(S["x1_step"], 1)

            def slot_stats(u, o=None, n=None, y=None):
                last = None
                if o is not None:
                    t, i = o
                    dve.wait_ge(S["a_o"], t + 1)
                    last = V.bn_stats(st3[:, u, O, :], o_sb[:, i, :])
                if n is not None:
                    last = V.bn_stats(st3[:, u, N, :], xt_(*n))
                if y is not None:
                    t, bt, i = y
                    wait_then_go(S["x1_step"], t + 1, 1)
                    last = V.bn_stats(st3[:, u, Y, :], xt_(bt, i))
                if last is not None:
                    last.then_inc(S["ln_step"], 1)

            def slot_aggr(s, u, which, count):
                wait_then_go(S["ln_step"], count)
                for k in which:
                    last = V.bn_aggr(mv3[:, u, k, :], st3[:, u, k, :])
                last.then_inc(S["ln_mv"], 1)

            def slot_apply(dst, src, u, k):
                return V.tensor_scalar(dst, src, mv3[:, u, k, 0:1], rstd3[:, u, k:k + 1], ALU.subtract, ALU.mult)

            def first_attention(bt, u, first=False, more=True, last=False):
                if more:
                    dve.wait_ge(S["x_ld"], DMA * (bt + 3))
                for i in range(TPB):
                    g = bt * TPB + i

                    def back(k):
                        if first and i < k:
                            return None
                        return (bt, i - k) if i >= k else (bt - 1, i - k + TPB)

                    dve.wait_ge(S["a_exp"], g + 1)
                    V.reciprocal(rinv[:, i % 2:i % 2 + 1], rowsum[:, i % 2:i % 2 + 1]).then_inc(S["a_rinv"], 1)
                    if not (last and i == TPB - 1):
                        first_rowmax(g + 1, (i + 1) % TPB)
                    if i >= 4:
                        dve.wait_ge(S["a_pt"], g + 1)
                        V.tensor_copy(pT[:, BANK:(i + 1) * P], bank(5, (i + 1) * P - BANK)).then_inc(S["a_pt_v"], 1)
                    o, y = back(1), back(4)
                    if more or o or y:
                        slot_stats(i % 2, o and (g - 1, o[1]), (bt + 2, i) if more else None, y and (g - 4, *y))
                    if back(3):
                        x1_sum(*back(3), g - 3)
                    if not last and i >= 6:
                        v_out(bt + 1, 1 - u, i - 6, 7)
                    normed = (bt + 2, i - 1) if i else (bt + 1, TPB - 1)
                    has_n = (more if i else not last and not first)
                    if has_n or back(5):
                        dve.wait_ge(S["ln_rs"], g)
                    if has_n:
                        if i in (1, 5):
                            dve.wait_ge(S["ch_ps"], 8 * (bt + 1) + (i + 3) // 4)
                        slot_apply(xn[:, normed[1], :], xt_(*normed), (i - 1) % 2, N).then_inc(S["a_xn"], 1)
                    if back(5):
                        slot_apply(yt_(*back(5)), xt_(*back(5)), (i - 1) % 2, Y).then_inc(S["a_y"], 1)
                    which = [k for k, has in ((O, o), (N, more), (Y, y)) if has]
                    slot_aggr(g, i % 2, which, g + 1)

            first_rowmax(0, 0)
            first_attention(0, 0, first=True)
            first_attention(1, 1)
            with dve.Fori(1, BATCH // 2 - 1) as p:
                first_attention(2 * p, 0)
                first_attention(2 * p + 1, 1)
            first_attention(BATCH - 2, 0, more=False)
            first_attention(BATCH - 1, 1, more=False, last=True)
            attention_weights_high(0)
            dve.wait_ge(S["a_y"], 2 * TPB)
            dve.sem_inc(S["h_go"], 1)
            T, B1 = TILES, BATCH - 1
            slot_stats(0, (T - 1, TPB - 1), None, (T - 4, B1, TPB - 4))
            V.memset(wkT[:, 0, :, 0:WINDOW], 0.0).then_inc(S["dve_step"], 1)
            V.memset(wvs[0:WINDOW, 0, :], 0.0).then_inc(S["dve_step"], 1)
            for k in (3, 2):
                x1_sum(B1, TPB - k, T - k)
            dve.wait_ge(S["ln_rs"], T)
            slot_apply(yt_(B1, TPB - 5), xt_(B1, TPB - 5), 1, Y).then_inc(S["a_y"], 1)
            slot_aggr(T, 0, (O, Y), T + 1)
            dve.wait_ge(S["dve_step"], 2)
            dve.sem_inc(S["stream"], 1)
            dve.wait_ge(S["consts"], DMA)
            rotation_tables()
            x1_sum(B1, TPB - 1, T - 1)
            dve.wait_ge(S["ln_rs"], T + 1)
            slot_apply(yt_(B1, TPB - 4), xt_(B1, TPB - 4), 0, Y).then_inc(S["a_y"], 1)
            wait_then_go(S["x1_step"], T, 1)
            for k, at in ((3, Y), (2, N), (1, O)):
                last = V.bn_stats(st3[:, 1, at, :], xt_(B1, TPB - k))
            last.then_inc(S["ln_step"], 1)
            slot_aggr(T + 1, 1, (O, N, Y), T + 2)
            attention_weights_low(0)
            dve.wait_ge(S["ln_rs"], T + 2)
            for k, at in ((3, Y), (2, N), (1, O)):
                slot_apply(yt_(B1, TPB - k), xt_(B1, TPB - k), 1, at).then_inc(S["a_y"], 1)
            dve.wait_ge(S["a_y"], TILES)

            with dve.Fori(0, DEPTH) as l:
                dve.wait_ge(S["tab_ok"], l + 1)

                def ff_weights():
                    dve.wait_ge(S["wf_ld"], DMA * WF_LOADS * (l + 1))
                    V.tensor_copy(w_1_hi[:], w_1[:]).then_inc(S["wf_hi"], 1)
                    dve.wait_ge(S["wf_hi"], l + 1)
                    V.tensor_tensor(w_1_lo[:], w_1[:], w_1_hi[:].bitcast(f32), ALU.subtract).then_inc(S["wf_lo"], 1)

                def h_low(t):
                    dve.wait_ge(S["h_hi"], l * TILES + t + 1)
                    V.tensor_tensor(hT_lo[:], bank(2, P), hT_hi[:].bitcast(f32), ALU.subtract).then_inc(S["h_t"], 1)

                def sumsq(t):
                    G = l * TILES + t
                    dve.wait_ge(S["sq_ok"], 2 * G + 2)
                    V.tensor_reduce(ss[:], sq.rearrange("p (h d) -> p h d", d=DH), AX.X, ALU.add).then_inc(S["ss_sum"], 1)
                    dve.wait_ge(S["ss_sum"], G + 1)
                    V.tensor_scalar(ss[:], ss[:], NORM_MIN2, None, ALU.max).then_inc(S["ss_ok"], 1)

                def rotate(t, first=False):
                    G = l * TILES + t
                    if not first:
                        dve.wait_ge(S["rot_sum"], G)
                    i = (t & (TPB - 1)) if not isinstance(t, int) else t % TPB

                    def split(a):
                        return a.rearrange("p (s h d) -> p s h d", s=2, d=DH)

                    tb = tab[:, bass.ds(i, 1), :, :].rearrange("p a s d -> p (a s) d")
                    qk = PS[:, 0:2 * BANK]
                    V.tensor_tensor(split(termA), split(qk), tb[:, 0:2, :].unsqueeze(2).broadcast_to([P, 2, HEADS, DH]), ALU.mult)
                    for h in range(2):
                        o, f = h * HALF, (1 - h) * HALF
                        last = V.tensor_tensor(split(termB)[:, :, :, o:o + HALF], split(qk)[:, :, :, f:f + HALF],
                                               tb[:, 2:4, o:o + HALF].unsqueeze(2).broadcast_to([P, 2, HEADS, HALF]), ALU.mult)
                    last.then_inc(S["rot_terms"], 1)

                def normalize(t, first):
                    G = l * TILES + t
                    dve.wait_ge(S["rot_sum"], G + 1)
                    dve.wait_ge(S["rr_ok"], G + 1)
                    if not first:
                        dve.wait_ge(S["k_turned"], G)
                    V.tensor_tensor(qk_rot.rearrange("p (h d) -> p h d", d=DH), rsum.rearrange("p (h d) -> p h d", d=DH),
                                    rr[:].unsqueeze(2).broadcast_to([P, 2 * HEADS, DH]), ALU.mult).then_inc(S["qk_ok"], 1)

                def rowmax(t, half):
                    G = l * TILES + t
                    dve.wait_ge(S["sc_ps"], 2 * G + half + 1)
                    V.tensor_reduce(wnegmax[:, 4 * half:4 * half + 4], bank(3 + half).rearrange("p (h c) -> p h c", c=P),
                                    AX.X, ALU.max, negate=True).then_inc(S["nm_ok"], 1)

                def probs_norm(t, u, half):
                    G, c = l * TILES + t, slice(4 * half, 4 * half + 4)
                    dve.wait_ge(S["probs"], 2 * G + half + 1)
                    V.reciprocal(wrinv[:, c], wrowsum[:, u, c]).then_inc(S["rinv_ok"], 1)
                    dve.wait_ge(S["rinv_ok"], 2 * G + half + 1)
                    V.tensor_tensor(wprob[:, c, :], wprob[:, c, :], wrinv[:, c].unsqueeze(2).broadcast_to([P, 4, P]),
                                    ALU.mult).then_inc(S["pn_ok"], 1)

                def residual(t):
                    G = l * TILES + t
                    dve.wait_ge(S["wo_ps"], G + 1)
                    yt = ys[:, bass.ds(yslot(t), 1), :].rearrange("p a c -> p (a c)")
                    V.tensor_tensor(yt, yt, bank(7, DIM), ALU.add).then_inc(S["updated"], 1)

                def slot(t, u, before=True, after=2):
                    rowmax(t, 0)
                    if after >= 2:
                        h_low(t + 2)
                    rowmax(t, 1)
                    probs_norm(t, u, 0)
                    if after >= 1:
                        normalize(t + 1, False)
                    probs_norm(t, u, 1)
                    if before:
                        residual(t - 1)
                    if after >= 2:
                        sumsq(t + 2)
                        rotate(t + 2)

                h_low(0)
                sumsq(0)
                rotate(0, first=True)
                h_low(1)
                normalize(0, True)
                sumsq(1)
                rotate(1)
                slot(0, 0, before=False)
                ff_weights()
                with dve.Fori(0, TILES // 2 - 2) as p:
                    slot(2 * p + 1, 1)
                    slot(2 * p + 2, 0)
                slot(TILES - 3, 1)
                slot(TILES - 2, 0, after=1)
                def group_stats(g, gu):
                    wait_then_go(*group_loaded(l, g, gu))
                    stats(fmv, fst, lambda i: hc[:, gu, i, :], GT, l * GROUPS + g).then_inc(S["c_mv"], 1)

                def group_norm(g, gu):
                    dve.wait_ge(S["c_rs"], l * GROUPS + g + 1)
                    for i in range(GT):
                        last = V.tensor_scalar(hc[:, gu, i, :], hc[:, gu, i, :], fmv[:, i, 0:1], frs[:, i:i + 1],
                                               ALU.subtract, ALU.mult)
                    last.then_inc(S["c_hn"], 1)

                def group_low(g):
                    dve.wait_ge(S["c_hi"], l * GROUPS + g + 1)
                    V.tensor_tensor(hcT_lo[:], hcT, hcT_hi[:].bitcast(f32), ALU.subtract).then_inc(S["c_lo"], 1)

                group_stats(0, 0)
                rowmax(TILES - 1, 0)
                rowmax(TILES - 1, 1)
                probs_norm(TILES - 1, 1, 0)
                probs_norm(TILES - 1, 1, 1)
                residual(TILES - 2)
                group_norm(0, 0)
                V.memset(hid_tail[64:P], 1.0).then_inc(S["ones"], 1)
                group_low(0)
                residual(TILES - 1)
                dve.wait_ge(S["updated"], (l + 1) * TILES)
                dve.wait_ge(S["ones"], l + 1)
                dve.sem_inc(S["stream"], 1)

                def gate(g, gu, m):
                    o, n = HBLK[m]
                    dve.wait_ge(S["c_gel"], NB * (l * GROUPS + g) + m + 1)
                    V.scalar_tensor_tensor(out=hidden(gu, m)[0:n], in0=bank(2 + m)[0:n], scalar=b_1[0:n, 0, m:m + 1],
                                           in1=gel[0:n, m, :], op0=ALU.add, op1=ALU.mult).then_inc(S["c_hid"], 1)

                def group_residual(g, gu, end=False):
                    G = l * GROUPS + g
                    dve.wait_ge(S["c_out_ps"], G + 1)
                    if not end:
                        dve.wait_ge(*group_loaded(l, g + 1, 1 - gu))
                    s = (g >> 1) * (TPB + 1) + 1 + gu * GT
                    if not isinstance(g, int):
                        s = bounded(s, 1, BATCH * (TPB + 1) - GT)
                    yg = ys[:, bass.ds(s, GT), :]
                    V.tensor_tensor(yg, yg, bank(gu).rearrange("p (i c) -> p i c", c=DIM), ALU.add).then_inc(S["c_out_free"], 1)

                def gslot(g, gu, first=False, after=2):
                    gate(g, gu, 0)
                    if after >= 1:
                        group_norm(g + 1, 1 - gu)
                    gate(g, gu, 1)
                    gate(g, gu, 2)
                    if after >= 1:
                        group_low(g + 1)
                    if after >= 2:
                        group_stats(g + 2, gu)
                    if not first:
                        group_residual(g - 1, 1 - gu)

                group_stats(1, 1)
                gslot(0, 0, first=True)
                with dve.Fori(0, GROUPS // 2 - 2) as p:
                    gslot(2 * p + 1, 1)
                    gslot(2 * p + 2, 0)
                gslot(GROUPS - 3, 1)
                dve.wait_ge(S["c_out_free"], 2 + l * GROUPS + 1)
                dve.sem_inc(S["h_go"], 1)
                gslot(GROUPS - 2, 0, after=1)
                attention_weights_high(l + 1)
                rotation_tables()
                gslot(GROUPS - 1, 1, after=0)
                attention_weights_low(l + 1)
                group_residual(GROUPS - 1, 1, end=True)
                dve.wait_ge(S["c_out_free"], 2 + (l + 1) * GROUPS)
                dve.sem_inc(S["stream"], 1)

            E0 = 2

            def last_stats(n):
                for i in range(TPB):
                    last = V.bn_stats(st2[:, n, i, :], ys[:, n * (TPB + 1) + 1 + i, :])
                last.then_inc(S["dve_step"], 1)

            def last_aggr(n):
                wait_then_go(S["dve_step"], E0 + n + 1, n % 2)
                for i in range(TPB):
                    last = V.bn_aggr(mv2[:, n, i, :], st2[:, n, i, :])
                last.then_inc(S["d_mv"], 1)

            for n in range(BATCH + 2):
                if n < BATCH:
                    last_stats(n)
                    last_aggr(n)
                if n >= 2:
                    m = n - 2
                    dve.wait_ge(S["d_app"], m + 1)
                    c = slice(0, LAST_DVE)
                    V.tensor_tensor(res[:, m, c], res[:, m, c],
                                    xs[:, m * TPB:(m + 1) * TPB, :].rearrange("p i c -> p (i c)")[:, c], ALU.add).then_inc(S["d_nrm"], 1)

        @block.tensor
        def _(pe):
            def three_passes(o, a_hi, a_lo, b_hi, b_lo):
                mm(o, a_hi, b_hi, start=True, stop=False)
                mm(o, a_hi, b_lo, start=False, stop=False)
                return mm(o, a_lo, b_hi, start=False, stop=True)

            pe.wait_ge(S["zeroed"], 5)
            pe.wait_ge(S["w_in_ld"], 3 * DMA)

            def piece(q, u, j, ps, alone=False):
                h = j % 2
                if j < 2:
                    pe.wait_ge(S["a_xn"], TPB * q + 4 * (j + 1))
                    if not alone:
                        pe.wait_ge(*((S["ch_a"], 6 * q + 1) if j else (S["ch_v"], 2 * q)))
                    for i in range(4):
                        done = tr(bank(ps, P, i * P), xn[:, 4 * j + i, :], ident[:])
                elif j < 6:
                    if not alone or j == 2:
                        pe.wait_ge(S["ch_a"], 6 * q + j)
                    s = (j - 2) // 2
                    done = mm(bank(ps), w_in[:, s * DIM:(s + 1) * DIM], xT[:, h * BANK:(h + 1) * BANK],
                              start=True, stop=True)
                else:
                    if not alone:
                        pe.wait_ge(*((S["ch_v"], 2 * q + 1) if h else (S["ch_a"], 6 * q + 6)))
                    for i in range(4):
                        done = mm(bank(ps, DIM, i * DIM), xT[:, (4 * h + i) * P:(4 * h + i + 1) * P],
                                  w_in[:, 2 * DIM:3 * DIM], start=True, stop=True)
                done.then_inc(S["ch_ps"], 1)

            def first_scores(g, i, u, early=False):
                if not early:
                    pe.wait_ge(S["a_exp"], g - 1)
                n, b0 = (i + 1) * P, (i % 2) * 2 * BANK
                for c in range(0, n, BANK):
                    w = min(BANK, n - c)
                    mm(PS[:, b0 + c:b0 + c + w], qT[:, u, i * P:(i + 1) * P], kT[:, u, c:c + w],
                       start=True, stop=c + w < n)
                mm(PS[:, b0 + i * P:b0 + n], identb[:], causal[:], start=False, stop=True).then_inc(S["a_sc"], 1)

            def first_attention(bt, u, first=False, last=False):
                for i in range(TPB):
                    g = bt * TPB + i
                    if i + 1 < TPB:
                        first_scores(g + 1, i + 1, u, early=first and i == 0)
                    elif not last:
                        pe.wait_ge(S["ch_a"], 6 * (bt + 1) + 6)
                        first_scores(g + 1, 0, 1 - u)
                    pe.wait_ge(S["a_exp"], g + 1)
                    for j in range(i + 1):
                        done = tr(bank(4 + j // 4, P, (j % 4) * P), prob[:, i % 2, j * P:(j + 1) * P], ident[:])
                    done.then_inc(S["a_pt"], 1)
                    if not last:
                        piece(bt + 1, 1 - u, i, 7)
                    if i == 0:
                        pe.wait_ge(S["ch_v"], 2 * bt + 2)
                    pe.wait_ge(S["a_pt_a"], g + 1)
                    if i >= 4:
                        pe.wait_ge(S["a_pt_v"], bt * 4 + i - 3)
                    if not (first and i == 0):
                        pe.wait_ge(S["a_o"], g)
                    for j in range(i + 1):
                        done = mm(bank(6, DIM), pT[:, j * P:(j + 1) * P], v_sb[:, u, j * DIM:(j + 1) * DIM],
                                  start=(j == 0), stop=(j == i))
                    done.then_inc(S["a_pv"], 1)

            for j in range(8):
                piece(0, 0, j, j, alone=True)
            pe.wait_ge(S["ch_a"], 6)
            first_scores(0, 0, 0, early=True)
            first_attention(0, 0, first=True)
            first_attention(1, 1)
            with pe.Fori(1, BATCH // 2 - 1) as p:
                first_attention(2 * p, 0)
                first_attention(2 * p + 1, 1)
            first_attention(BATCH - 2, 0)
            first_attention(BATCH - 1, 1, last=True)

            with pe.Fori(0, DEPTH) as l:
                pe.wait_ge(S["wa_lo"], l + 1)

                def xt(t, u, first):
                    G = l * TILES + t
                    pe.wait_ge(*h_loaded(l, t, u))
                    if not first:
                        pe.wait_ge(S["v_ok"], G)
                    tr(bank(2, P), h_in[:, u, :], ident[:]).then_inc(S["xt_ps"], 1)

                def qkv(t, first):
                    G = l * TILES + t
                    pe.wait_ge(S["h_t"], G + 1)
                    if not first:
                        pe.wait_ge(S["rot_terms"], G)
                    for n, done in enumerate(("q_ps", "k_ps", "v_ps")):
                        c = slice(n * INNER, (n + 1) * INNER)
                        three_passes(bank(n), hT_hi[:], hT_lo[:], w_qkv_hi[:, c], w_qkv_lo[:, c]).then_inc(S[done], 1)

                def turn_qk(t, s):
                    pe.wait_ge(S["qk_ok"], l * TILES + t + 1)
                    for c in range(INNER // P):
                        last = tr(bank(5 + s, P, c * P), qk_rot[:, s * INNER + c * P:s * INNER + (c + 1) * P], ident[:])
                    last.then_inc(S["k_turned" if s else "q_turned"], 1)

                def turn_probs(t, half):
                    pe.wait_ge(S["pn_ok"], 2 * (l * TILES + t) + half + 1)
                    for j in range(half * 4, half * 4 + 4):
                        last = tr(bank(3 + half, P, (j % 4) * P), wprob[:, j, :], ident[:])
                    last.then_inc(S["pt_ps"], 1)

                def values(t, k, half, before):
                    G, u = l * TILES + t, k % 2
                    pe.wait_ge(S["pt_ok"], 2 * G + half + 1)
                    if not half:
                        pe.wait_ge(*hi_shifted(l, t, u))
                        if before:
                            pe.wait_ge(*lo_shifted(l, t - 1, 1 - u))
                            pe.wait_ge(S["updated"], G)
                    for j in range(4 * half, 4 * half + 4):
                        h = head(j)
                        c, rows = slice(h * DH, (h + 1) * DH), slice(half * DH, (half + 1) * DH)
                        o = bank(7, P, (h // 2) * P)
                        mm(o[rows, 0:WINDOW], wvs[:, u, c], wpT[:, j, 0:WINDOW], start=True, stop=True)
                        last = mm(o[rows, WINDOW:P], wv[:, k, c], wpT[:, j, WINDOW:P], start=True, stop=True)
                    if half:
                        last.then_inc(S["o_ps"], 1)

                def wscores(t, u, half):
                    G = l * TILES + t
                    pe.wait_ge(S["qk_t"], G + 1)
                    if isinstance(t, int):
                        msk = band[:, 0 if t % TPB == 0 else 1, :]
                    else:
                        sel = bounded(((t & (TPB - 1)) + (TPB - 1)) >> 3, 0, 1)
                        msk = band[:, bass.ds(sel, 1), :].rearrange("p a c -> p (a c)")
                    mm(bank(3 + half), identb[:], msk, start=True, stop=False)
                    for j in range(half * 4, half * 4 + 4):
                        h = head(j)
                        r, g = slice((h % 2) * DH, (h % 2 + 1) * DH), h // 2
                        o = bank(3 + half, P, (j % 4) * P)
                        mm(o[0:WINDOW], wqT[r, g, 0:WINDOW], wkT[r, u, g, 0:P], start=False, stop=(j % 4 == 3))
                        last = mm(o[WINDOW:P], wqT[r, g, WINDOW:P], wkT[r, u, g, WINDOW:], start=False, stop=(j % 4 == 3))
                    last.then_inc(S["sc_ps"], 1)

                def project(t):
                    pe.wait_ge(S["ot_ok"], l * TILES + t + 1)
                    for c in range(INNER // P):
                        last = mm(bank(7, DIM), oT[:, c, :], w_o[:, c, :], start=(c == 0), stop=(c == INNER // P - 1))
                    last.then_inc(S["wo_ps"], 1)

                def slot(t, k, before=True, after=2):
                    u = k % 2
                    wscores(t, u, 0)
                    if after >= 2:
                        xt(t + 2, u, False)
                    wscores(t, u, 1)
                    if after >= 2:
                        qkv(t + 2, False)
                    if before:
                        project(t - 1)
                    turn_probs(t, 0)
                    if after >= 1:
                        turn_qk(t + 1, 0)
                    turn_probs(t, 1)
                    if after >= 1:
                        turn_qk(t + 1, 1)
                    values(t, k, 0, before)
                    values(t, k, 1, before)

                xt(0, 0, True)
                pe.wait_ge(S["stream"], 2 * l + 1)
                qkv(0, True)
                xt(1, 1, False)
                qkv(1, False)
                turn_qk(0, 0)
                turn_qk(0, 1)
                slot(0, 0, before=False)
                with pe.Fori(0, TILES // 4 - 1) as p:
                    for k in (1, 2, 3, 4):
                        slot(4 * p + k, k % 4)
                slot(TILES - 3, 1)
                slot(TILES - 2, 2, after=1)
                def turn_h(g, gu, first=False):
                    G = l * GROUPS + g
                    pe.wait_ge(S["c_hn"], G + 1)
                    if not first:
                        pe.wait_ge(S["c_hid"], NB * (G - 1) + 1)
                    for i in range(GT):
                        last = tr(bank(2, P, i * P), hc[:, gu, i, :], ident[:])
                    last.then_inc(S["c_t_ps"], 1)

                wscores(TILES - 1, 1, 0)
                wscores(TILES - 1, 1, 1)
                project(TILES - 2)
                turn_probs(TILES - 1, 0)
                turn_probs(TILES - 1, 1)
                values(TILES - 1, 3, 0, True)
                values(TILES - 1, 3, 1, True)
                pe.wait_ge(S["v_ok"], (l + 1) * TILES)
                turn_h(0, 0, first=True)
                project(TILES - 1)

                pe.wait_ge(S["stream"], 2 * l + 2)
                pe.wait_ge(S["wf_lo"], l + 1)

                def up(g, gu, first=False):
                    G = l * GROUPS + g
                    pe.wait_ge(S["c_lo"], G + 1)
                    for m, (o, n) in enumerate(HBLK):
                        if not first:
                            pe.wait_ge(S["c_hid"], NB * (G - 1) + m + 1)
                        for b0, c0 in ((2, o), (5, HID + o)):
                            last = three_passes(bank(b0 + m)[0:n], w_1_hi[:, c0:c0 + n], w_1_lo[:, c0:c0 + n],
                                                hcT_hi[:], hcT_lo[:])
                        last.then_inc(S["c_g_ps"], 1)

                def down(g, gu):
                    G = l * GROUPS + g
                    pe.wait_ge(S["c_hid"], NB * (G + 1))
                    pe.wait_ge(S["c_out_free"], G + 1)
                    for i in range(GT):
                        for m, (o, n) in enumerate(HBLK):
                            n += m == NB - 1
                            last = mm(bank(gu, DIM, i * DIM), hidden(gu, m)[0:n, i * P:(i + 1) * P], w_2[0:n, m, :],
                                      start=(m == 0), stop=(m == NB - 1))
                    last.then_inc(S["c_out_ps"], 1)

                def gslot(g, gu, first=False, last=False):
                    up(g, gu, first)
                    if not last:
                        turn_h(g + 1, 1 - gu)
                    if not first:
                        down(g - 1, 1 - gu)

                gslot(0, 0, first=True)
                with pe.Fori(0, GROUPS // 2 - 1) as p:
                    gslot(2 * p + 1, 1)
                    gslot(2 * p + 2, 0)
                gslot(GROUPS - 1, 1, last=True)
                down(GROUPS - 1, 1)


_INS = ['L0_attn_x', 'L0_attn_W', 'L0_attn_b', 'L0_ffn_wqkv', 'L0_ffn_q_scale', 'L0_ffn_k_scale', 'L0_ffn_wo',
        'L0_ffn_ln_g', 'L0_ffn_ln_b', 'L0_ffn_w1', 'L0_ffn_b1', 'L0_ffn_w2', 'L0_ffn_b2']


def xpos_tables():
    import numpy as np
    f = np.float32
    half_idx = np.arange(0, DH, 2, dtype=f)
    inv_freq = (f(1.0) / np.power(f(10000.0), half_idx / f(DH))).astype(f)
    t = np.arange(SEQ, dtype=f)
    freqs = t[:, None] * inv_freq[None, :]
    base = (half_idx + f(0.4 * DH)) / f(1.4 * DH)
    power = (t - f(SEQ // 2)) / f(WINDOW // 2)
    scale = np.power(base[None, :], power[:, None]).astype(f)
    cos, sin = np.cos(freqs).astype(f), np.sin(freqs).astype(f)
    q8 = f(QK_SCALE)
    rows = [np.concatenate([cos * scale * q8] * 2, -1), np.concatenate([cos / scale] * 2, -1),
            np.concatenate([-sin * scale * q8, sin * scale * q8], -1), np.concatenate([-sin / scale, sin / scale], -1)]
    tab = np.stack(rows, 1).astype(f)
    return np.ascontiguousarray(tab.reshape(TPB, P, 4, DH).transpose(1, 0, 2, 3))


def kernel(**inputs):
    import numpy as _np
    import concourse.bacc as _bacc
    from concourse.bass_utils import run_bass_kernel_spmd as _run

    nc = _bacc.Bacc("TRN2", target_bir_lowering=False, num_devices=1)
    arrays, args = {}, []
    for name in _INS:
        a = _np.ascontiguousarray(inputs[name])
        arrays[f"in_{name}"] = a
        args.append(nc.dram_tensor(f"in_{name}", a.shape, mybir.dt.from_np(a.dtype), kind="ExternalInput").ap())
    tables = xpos_tables()
    arrays["xpos"] = tables
    args.append(nc.dram_tensor("xpos", tables.shape, mybir.dt.from_np(tables.dtype), kind="ExternalInput").ap())
    out = nc.dram_tensor("out_0", (BATCH, SEQ, DIM), mybir.dt.float32, kind="ExternalOutput").ap()
    build_program(nc, *args, out)
    r = _run(nc, [arrays], core_ids=[0])
    return r.results[0]["out_0"]
```
